# Optimizing a Trainium2 kernel written in Bass

```python
import numpy as np
import jax
import jax.numpy as jnp

def _softmax(x, axis=-1):
    return jax.nn.softmax(x, axis=axis)

def _gelu(x):
    return jax.nn.gelu(x, approximate=True)

def _silu(x):
    return jax.nn.silu(x)

def _sigmoid(x):
    return jax.nn.sigmoid(x)

def _layernorm(x, axis=-1, eps=1e-05):
    m = jnp.mean(x, axis=axis, keepdims=True)
    v = jnp.var(x, axis=axis, keepdims=True)
    return (x - m) / jnp.sqrt(v + eps)

def _scatter_add(tgt, idx, src, axis=0):
    return tgt.at[idx].add(src)

def _segment_sum(src, seg, n):
    return jax.ops.segment_sum(src, seg, n)
kernel_name = 'mk_flamingo_gated_d1_seqx_r4_d9e327'

def setup_inputs(seed: int=0):
    np.random.seed(seed)
    _w = jnp.asarray

    def _rec_inputs():
        import jax
        import jax.numpy as jnp
        _rk = jax.random.key(seed)
        x = -0.0002928 + 1 * jax.random.normal(jax.random.fold_in(_rk, 1), (16, 512, 256), jnp.float32)
        _lenS = 512 - jax.random.randint(jax.random.fold_in(_rk, 7), (16,), 0, max(1, 512 // 4) + 1, jnp.int32)
        _lenS2 = 64 - jax.random.randint(jax.random.fold_in(_rk, 8), (16,), 0, max(1, 64 // 4) + 1, jnp.int32)
        _ctx_512P = jax.random.normal(jax.random.fold_in(_rk, 11), (16, 16, 128), jnp.float32)
        _ctx_512c = jax.random.dirichlet(jax.random.fold_in(_rk, 511), 0.3 * jnp.ones((16,), jnp.float32), (16, 64))
        _ctx_512t = jnp.einsum('bsk,bkd->bsd', _ctx_512c, _ctx_512P)
        _ctx_512t = _ctx_512t * jax.lax.rsqrt(jnp.mean(jnp.square(_ctx_512t)) + 1e-12) * 0.953939
        ctx_512 = 0.00222621 + 0.99962 * (_ctx_512t + 0.3 * jax.random.normal(jax.random.fold_in(_rk, 611), (16, 64, 128), jnp.float32))
        _g = jax.random.normal(jax.random.fold_in(_rk, 9001), (2, 1), jnp.float32)
        _g = jnp.sign(_g) * jnp.maximum(jnp.abs(_g), 1.0) + (_g == 0) * 1.0
        g_xattn = _g[0]
        g_ffn = _g[1]
        return (x, ctx_512, g_xattn, g_ffn)
    x, ctx_512, g_xattn, g_ffn = _rec_inputs()

    def _L0_xattn_setup():
        import jax, jax.numpy as jnp
        import numpy as np
        B, T, TC, C, CC, H = (2, 512, 128, 256, 128, 16)
        D = C // H

        def _heads(t):
            b, l, _ = t.shape
            return t.reshape(b, l, H, D).transpose(0, 2, 1, 3)
        key = jax.random.key(seed)
        ks = jax.random.split(key, 18)
        w = lambda k, i, o: jax.random.normal(k, (i, o), jnp.float32) / np.sqrt(i).astype(np.float32)
        return {'x': jax.random.normal(ks[0], (B, T, C), jnp.float32), 'cross_input': jax.random.normal(ks[1], (B, TC, CC), jnp.float32), 'Wk': w(ks[2], C, C), 'bk': jnp.zeros((C,), jnp.float32), 'Wq': w(ks[3], C, C), 'bq': jnp.zeros((C,), jnp.float32), 'Wv': w(ks[4], C, C), 'bv': jnp.zeros((C,), jnp.float32), 'Wck': w(ks[5], CC, C), 'bck': jnp.zeros((C,), jnp.float32), 'Wcq': w(ks[6], C, C), 'bcq': jnp.zeros((C,), jnp.float32), 'Wcv': w(ks[7], CC, C), 'bcv': jnp.zeros((C,), jnp.float32), 'Wp': w(ks[8], C, C), 'bp': jnp.zeros((C,), jnp.float32)}
    _L0_xattn_all = _L0_xattn_setup()
    _L0_xattn_in = {k: v for k, v in _L0_xattn_all.items() if k in ('Wk', 'bk', 'Wq', 'bq', 'Wv', 'bv', 'Wck', 'bck', 'Wcq', 'bcq', 'Wcv', 'bcv', 'Wp', 'bp')}
    del _L0_xattn_all

    def _L0_ffn_setup():
        import jax, jax.numpy as jnp
        import numpy as np
        B, S, H, I, E, TOPK, KS = (4, 1024, 256, 128, 16, 2, 3)
        key = jax.random.key(seed)
        ks = jax.random.split(key, 9)
        sc = 0.02
        return {'hidden_states': jax.random.normal(ks[0], (B, S, H), dtype=jnp.float32), 'router_w': jax.random.normal(ks[1], (H, E), dtype=jnp.float32) * sc, 'router_bias': jnp.zeros((E,), dtype=jnp.float32), 'expert_gate_w': jax.random.normal(ks[2], (E - 1, H, I), dtype=jnp.float32) * sc, 'expert_up_w': jax.random.normal(ks[3], (E - 1, H, I), dtype=jnp.float32) * sc, 'expert_down_w': jax.random.normal(ks[4], (E - 1, I, H), dtype=jnp.float32) * sc, 'conv_w': jax.random.normal(ks[5], (I, H, KS), dtype=jnp.float32) * sc, 'shared_up_w': jax.random.normal(ks[6], (H, I), dtype=jnp.float32) * sc, 'shared_down_w': jax.random.normal(ks[7], (I, H), dtype=jnp.float32) * sc}
    _L0_ffn_all = _L0_ffn_setup()
    _L0_ffn_in = {k: v for k, v in _L0_ffn_all.items() if k in ('router_w', 'router_bias', 'expert_gate_w', 'expert_up_w', 'expert_down_w', 'conv_w', 'shared_up_w', 'shared_down_w')}
    del _L0_ffn_all
    return {'x': x, 'ctx_512': ctx_512, 'g_xattn': g_xattn, 'g_ffn': g_ffn, 'L0_xattn_Wk': _L0_xattn_in['Wk'], 'L0_xattn_bk': _L0_xattn_in['bk'], 'L0_xattn_Wq': _L0_xattn_in['Wq'], 'L0_xattn_bq': _L0_xattn_in['bq'], 'L0_xattn_Wv': _L0_xattn_in['Wv'], 'L0_xattn_bv': _L0_xattn_in['bv'], 'L0_xattn_Wck': _L0_xattn_in['Wck'], 'L0_xattn_bck': _L0_xattn_in['bck'], 'L0_xattn_Wcq': _L0_xattn_in['Wcq'], 'L0_xattn_bcq': _L0_xattn_in['bcq'], 'L0_xattn_Wcv': _L0_xattn_in['Wcv'], 'L0_xattn_bcv': _L0_xattn_in['bcv'], 'L0_xattn_Wp': _L0_xattn_in['Wp'], 'L0_xattn_bp': _L0_xattn_in['bp'], 'L0_ffn_router_w': _L0_ffn_in['router_w'], 'L0_ffn_router_bias': _L0_ffn_in['router_bias'], 'L0_ffn_expert_gate_w': _L0_ffn_in['expert_gate_w'], 'L0_ffn_expert_up_w': _L0_ffn_in['expert_up_w'], 'L0_ffn_expert_down_w': _L0_ffn_in['expert_down_w'], 'L0_ffn_conv_w': _L0_ffn_in['conv_w'], 'L0_ffn_shared_up_w': _L0_ffn_in['shared_up_w'], 'L0_ffn_shared_down_w': _L0_ffn_in['shared_down_w']}

def reference(x, ctx_512, g_xattn, g_ffn, L0_xattn_Wk, L0_xattn_bk, L0_xattn_Wq, L0_xattn_bq, L0_xattn_Wv, L0_xattn_bv, L0_xattn_Wck, L0_xattn_bck, L0_xattn_Wcq, L0_xattn_bcq, L0_xattn_Wcv, L0_xattn_bcv, L0_xattn_Wp, L0_xattn_bp, L0_ffn_router_w, L0_ffn_router_bias, L0_ffn_expert_gate_w, L0_ffn_expert_up_w, L0_ffn_expert_down_w, L0_ffn_conv_w, L0_ffn_shared_up_w, L0_ffn_shared_down_w):
    import jax
    import jax.numpy as jnp

    def _L0_xattn_ref(x, cross_input, Wk, bk, Wq, bq, Wv, bv, Wck, bck, Wcq, bcq, Wcv, bcv, Wp, bp):
        import jax, jax.numpy as jnp
        import numpy as np
        B, T, TC, C, CC, H = (2, 512, 128, 256, 128, 16)
        D = C // H

        def _heads(t):
            b, l, _ = t.shape
            return t.reshape(b, l, H, D).transpose(0, 2, 1, 3)
        scale = np.float32(1.0 / np.sqrt(D))
        q = _heads(x @ Wq + bq)
        k = _heads(x @ Wk + bk)
        v = _heads(x @ Wv + bv)
        att = jnp.einsum('bhqd,bhkd->bhqk', q, k) * scale
        causal = jnp.tril(jnp.ones((T, T), bool))
        att = jnp.where(causal[None, None], att, -jnp.inf)
        y = jnp.einsum('bhqk,bhkd->bhqd', jax.nn.softmax(att, axis=-1), v)
        qc = _heads(x @ Wcq + bcq)
        kc = _heads(cross_input @ Wck + bck)
        vc = _heads(cross_input @ Wcv + bcv)
        attc = jnp.einsum('bhqd,bhkd->bhqk', qc, kc) * scale
        y = y + jnp.einsum('bhqk,bhkd->bhqd', jax.nn.softmax(attc, axis=-1), vc)
        y = y.transpose(0, 2, 1, 3).reshape(x.shape[0], T, C)
        return y @ Wp + bp

    def _L0_ffn_ref(hidden_states, router_w, router_bias, expert_gate_w, expert_up_w, expert_down_w, conv_w, shared_up_w, shared_down_w):
        import jax, jax.numpy as jnp
        import numpy as np
        B, S, H, I, E, TOPK, KS = (4, 1024, 256, 128, 16, 2, 3)
        b, s, h = hidden_states.shape
        flat = hidden_states.reshape(b * s, h)
        logits = (flat @ router_w).astype(jnp.float32) + router_bias
        probs = jax.nn.softmax(logits, axis=-1)
        top_w, top_i = jax.lax.top_k(probs, TOPK)
        norm_w = top_w / (jnp.sum(top_w, axis=-1, keepdims=True) + 1e-06)
        norm_w = norm_w.astype(hidden_states.dtype)
        combine = jnp.sum(jax.nn.one_hot(top_i, E, dtype=norm_w.dtype) * norm_w[..., None], axis=1)
        routed = combine[:, E - 1:E] * flat
        for e in range(E - 1):
            y = jax.nn.silu(flat @ expert_gate_w[e]) * (flat @ expert_up_w[e]) @ expert_down_w[e]
            routed = routed + combine[:, e:e + 1] * y
        routed = routed.reshape(b, s, h)
        x_ncw = jnp.transpose(hidden_states, (0, 2, 1))
        gate = jax.lax.conv_general_dilated(x_ncw, conv_w, window_strides=(1,), padding=[(KS - 1, 0)], dimension_numbers=('NCW', 'OIW', 'NCW'))
        gate = jnp.transpose(gate, (0, 2, 1))
        shared = jax.nn.silu(gate) * (hidden_states @ shared_up_w) @ shared_down_w
        return shared + routed
    x = x + jnp.tanh(g_xattn[0]) * _L0_xattn_ref(_layernorm(x, axis=-1), ctx_512, L0_xattn_Wk, L0_xattn_bk, L0_xattn_Wq, L0_xattn_bq, L0_xattn_Wv, L0_xattn_bv, L0_xattn_Wck, L0_xattn_bck, L0_xattn_Wcq, L0_xattn_bcq, L0_xattn_Wcv, L0_xattn_bcv, L0_xattn_Wp, L0_xattn_bp)
    x = x + jnp.tanh(g_ffn[0]) * _L0_ffn_ref(_layernorm(x, axis=-1), L0_ffn_router_w, L0_ffn_router_bias, L0_ffn_expert_gate_w, L0_ffn_expert_up_w, L0_ffn_expert_down_w, L0_ffn_conv_w, L0_ffn_shared_up_w, L0_ffn_shared_down_w)
    return x

_drawn_inputs = setup_inputs


def setup_inputs(seed=0):
    import zlib

    import numpy as np

    out = dict(_drawn_inputs(seed))
    spreads = {'L0_xattn_bk': (0.0, 0.8),
     'L0_xattn_bq': (0.0, 0.395),
     'L0_xattn_bv': (0.0, 0.1),
     'L0_xattn_bck': (0.0, 0.8),
     'L0_xattn_bcq': (0.0, 0.271),
     'L0_xattn_bcv': (0.0, 0.1),
     'L0_xattn_bp': (0.0, 0.1),
     'L0_ffn_router_bias': (0.0, 0.1)}
    factors = {'L0_ffn_expert_gate_w': 7.894,
     'L0_ffn_expert_up_w': 7.792,
     'L0_ffn_expert_down_w': 7.789,
     'L0_ffn_conv_w': 3.067,
     'L0_ffn_shared_up_w': 2.946,
     'L0_ffn_shared_down_w': 2.954}
    for name, (base, spread) in spreads.items():
        noise = np.random.default_rng([zlib.crc32(name.encode()), seed]).standard_normal(out[name].shape)
        drawn = base * np.exp(spread * noise) if base else spread * noise
        out[name] = jnp.asarray(drawn.astype(out[name].dtype))
    for name, factor in factors.items():
        out[name] = (out[name] * factor).astype(out[name].dtype)
    return out
```

```python
from contextlib import ExitStack

import concourse.bass as bass
from concourse import mybir

ALU = mybir.AluOpType
ACT = mybir.ActivationFunctionType
F32 = mybir.dt.float32
BF16 = mybir.dt.bfloat16
I32 = mybir.dt.int32
U32 = mybir.dt.uint32
AX = mybir.AxisListType.X

P = 128
HEAD_GROUP = 4
BIG = 1.0e30
EPS = 1e-5


PARTS = {
    "pro": (False, False, True), "first": (False, True, True), "mid": (True, True, True),
    "last": (True, True, False), "post": (True, False, False),
}


class Events:

    def __init__(self, names, last_batch, credit=0):
        self.names = names
        self.last_batch = last_batch
        self.credit = credit

    def start(self, kind, b):
        n = {k: len(self.names(k)) for k in PARTS}
        if kind == "pro":
            return self.credit
        if kind == "first":
            return self.credit + n["pro"]
        if kind == "mid":
            return self.credit + n["pro"] + n["first"] + (b - 1) * n["mid"]
        end = self.credit + n["pro"] + n["first"] + (self.last_batch - 1) * n["mid"]
        return end if kind == "last" else end + n["last"]

    def upto(self, kind, b, name):
        return self.start(kind, b) + self.names(kind).index(name) + 1

    def slot(self, kind, name, ring):
        before = self.start(kind, 1) - self.credit
        return (before + self.names(kind).index(name)) % ring


def attention_phase(nc, x, ctx, g_xattn, W, x1s):
    B, T, C = x.shape
    TC, CC = ctx.shape[1:]
    H, D = 16, C // 16
    KC, QT = C // P, T // P
    HU = H // KC
    ALLC = 3 * T + TC
    Q0, CQ0, K0, KC0 = 0, T, 2 * T, 3 * T
    STACK, MROWS = 6 * D, 3
    SCALE = 1.0 / D ** 0.5
    RING = 3
    assert KC == 2 and QT == 4 and HU * D == P and 2 * TC == P and CC == P

    GROUP = [("X", 0), ("X", 1), ("A", 0), ("B", 0), ("A", 1), ("B", 1), ("C", 0),
             ("A", 2), ("B", 2), ("A", 3), ("B", 3), ("C", 2)]
    PT_SLOT = {n: i for i, n in enumerate(GROUP[2:])}
    NST = 2 * len(GROUP)
    MAXU = []
    for qt in range(QT):
        MAXU.append(("cross", qt, 0, HU))
        n = {0: 4, 1: 2, 2: 1, 3: 1}[qt]
        MAXU += [("self", qt, h, n) for h in range(0, HU, n)]
    NSM = len(MAXU)
    SM_LOOP, SM_MID = 20, 23

    def scalar_units(kind):
        prev, cur, nxt = PARTS[kind]
        out = []
        for c in range(KC):
            if nxt and c == 0:
                out += [("xT", t) for t in range(QT)]
            if nxt:
                out += [("proj", c, i) for i in range(4)]
            if cur:
                out += [("st", c, k) for k in range(NST)]
        return out

    def vector_units(kind):
        prev, cur, nxt = PARTS[kind]
        out = []
        if cur:
            out += [("v", 1), ("vc", 1)]
        if prev:
            out += [("tU", 1, 1, "x"), ("tU", 1, 1, "s")]
        if cur:
            out += [("mT", 0)]
        if prev:
            out += [("yT", k) for k in range(KC)] + [("wp", t) for t in range(QT)]
        if cur:
            out += [("sm", 1, k) for k in range(SM_MID)] + [("tU", 0, 0, "x"), ("tU", 0, 0, "s")]
            out += [("sm", 1, k) for k in range(SM_MID, NSM)]
        if nxt:
            out += [("v", 0), ("vc", 0)]
        if cur:
            out += [("tU", 0, 1, "x"), ("tU", 0, 1, "s"), ("mT", 1)]
        if nxt:
            out += [("sm", 0, k) for k in range(SM_MID)]
        if cur:
            out += [("tU", 1, 0, "x"), ("tU", 1, 0, "s")]
        if nxt:
            out += [("sm", 0, k) for k in range(SM_MID, NSM)]
        return out

    def of_current(names):
        return lambda kind: names if PARTS[kind][1] else []

    def of_next(names):
        return lambda kind: names if PARTS[kind][2] else []

    LB = B - 1
    SU, VU = Events(scalar_units, LB), Events(vector_units, LB)
    assert len(scalar_units("mid")) % RING == 0 and len(vector_units("mid")) % RING == 0
    PV = Events(of_current([(w, c, g) for c in range(KC) for g in range(2) for w in ("x", "s")]), LB, credit=8)
    MASKED = Events(of_current([(c, g, s) for c in range(KC) for g in range(2) for s in range(10)]), LB)
    YADD = Events(lambda kind: ([(1, 1)] if PARTS[kind][0] else []) + ([(0, 0), (0, 1), (1, 0)] if PARTS[kind][1] else []),
                  LB, credit=4)
    SPLIT = Events(of_next([0, 1]), LB)
    MSPLIT = Events(of_current([0, 1]), LB)
    LN = Events(of_next([0]), LB)

    scr = nc.dram_tensor("qk_scratch", (KC, 3, P, ALLC), BF16, kind="Internal").ap()
    mscr = nc.dram_tensor("max_scratch", (KC, 3, HU * 2 * T), BF16, kind="Internal").ap()

    with ExitStack() as st:
        def sb(name, shape, dt=F32):
            return st.enter_context(nc.sbuf_tensor(name, shape, dt))

        def sem(name):
            return st.enter_context(nc.semaphore(name))

        banks_s = [st.enter_context(nc.psum_tensor(f"scalar_bank{i}", [P, 512], F32)) for i in range(RING)]
        banks_v = [st.enter_context(nc.psum_tensor(f"vector_bank{i}", [P, 512], F32)) for i in range(RING)]
        pv_self = st.enter_context(nc.psum_tensor("pv_self", [P, 512], F32))
        pv_cross = st.enter_context(nc.psum_tensor("pv_cross", [P, 512], F32))

        wq = {n: sb(f"w_{n}", [P, KC, KC, P]) for n in ("q", "cq", "k")}
        wck = sb("w_ck", [P, KC, P])
        wv = sb("w_v", [P, KC, C])
        wcv = sb("w_cv", [P, C])
        wp = sb("w_p", [P, KC, C])
        bias_rows = sb("bias_rows", [8, P])
        bias_perm = sb("bias_perm", [8, P])
        bias = sb("bias", [P, 8])
        bv = sb("bv", [P, KC, QT, P])
        bcv = sb("bcv", [P, C])
        bpg = sb("bpg", [P, C])
        gate = sb("gate", [P, 1])
        ident = sb("ident", [P, P])
        ident_b = sb("ident_b", [P, P], BF16)
        tri = sb("tri", [P, 4, P], BF16)
        half = sb("half", [P, QT])

        xt = sb("xt", [P, QT, C])
        stats = sb("stats", [P, QT, 6])
        mv = sb("mv", [P, QT, 2])
        rstd = sb("rstd", [P, QT])
        xn = sb("xn", [P, QT, C])
        xnT = sb("xnT", [P, KC, T])
        ctile = sb("ctile", [P, CC])
        ctxT = sb("ctxT", [P, P])
        q32 = sb("q32", [P, ALLC])
        parts = sb("parts", [P, 3, ALLC], BF16)
        stack = [sb(f"stack{c}", [P, HU, ALLC], BF16) for c in range(KC)]
        vst = sb("vst", [P, QT, KC, HU, 32])
        vcst = sb("vcst", [P, KC, HU // 2, 64])
        nmax = [sb(f"nmax{c}", [P, QT, HU, 2]) for c in range(KC)]
        mres = sb("mres", [P, QT, HU * 2])
        mparts = sb("mparts", [P, QT, 3, HU * 2], BF16)
        mT = [sb(f"mT{c}", [3 * HU * 2, T], BF16) for c in range(KC)]
        pt = [sb(f"pt{g}", [P, 10, 512]) for g in range(2)]
        ct = [sb(f"ct{g}", [P, 2, 512]) for g in range(2)]
        usum = {(w, g): sb(f"usum_{w}{g}", [P, T]) for w in ("x", "s") for g in range(2)}
        recip = {w: sb(f"recip_{w}", [P, QT, HEAD_GROUP]) for w in ("x", "s")}
        y = sb("y", [P, QT, H, D])
        yc = [sb(f"yc{g}", [P, QT, HEAD_GROUP, D]) for g in range(2)]
        yT = sb("yT", [P, KC, T])
        xr = sb("xr", [P, QT, C])
        raw = {n: pt[0][:, i, :].rearrange("p (k c) -> p k c", k=KC) for i, n in enumerate(("q", "cq", "k"))}
        raw_ck = pt[0][:, 3, 0:C]

        passed = sem("passed")
        weights_in = sem("weights_in")
        setup_pool = sem("setup_pool")
        setup_vec = sem("setup_vec")
        setup_pe = sem("setup_pe")
        gate_ready = sem("gate_ready")
        scalar_filled = sem("scalar_filled")
        scalar_drained = sem("scalar_drained")
        vector_filled = sem("vector_filled")
        vector_drained = sem("vector_drained")
        pv_filled = sem("pv_filled")
        pv_drained = sem("pv_drained")
        norm_step = sem("norm_step")
        masked = sem("masked")
        y_added = sem("y_added")
        split_done = sem("split_done")
        h_ready = sem("h_ready")
        r_ready = sem("r_ready")
        m_ready = sem("m_ready")
        msplit_done = sem("msplit_done")
        msplit_step = sem("msplit_step")
        x_in = sem("x_in")
        ctx_in = sem("ctx_in")
        xr_in = sem("xr_in")
        xres_ready = sem("xres_ready")
        stats_ready = sem("stats_ready")
        mv_ready = sem("mv_ready")
        rstd_step = sem("rstd_step")
        rstd_ready = sem("rstd_ready")
        xn_ready = sem("xn_ready")
        scr_written = sem("scr_written")
        stack_in = [sem(f"stack_in{c}") for c in range(KC)]
        m_stored = sem("m_stored")
        m_in = [sem(f"m_in{c}") for c in range(KC)]
        x1_stored = sem("x1_stored")

        NW = 22
        block = st.enter_context(nc.Block())

        def over_batches(eng, body):
            body("pro", 0)
            body("first", 0)
            with eng.Fori(1, B - 1) as b:
                body("mid", b)
            body("last", B - 1)
            body("post", B)

        @block.sync
        def _(sp):
            def load_x(b):
                sp.dma_start(xt[:, :, :], x[b].rearrange("(t p) c -> p t c", p=P)).then_inc(x_in, 16)

            def load_ctx(b):
                for i in range(2):
                    sp.dma_start(ctile[i * TC:(i + 1) * TC, :], ctx[b]).then_inc(ctx_in, 16)

            def load_xr(b):
                sp.dma_start(xr[:, :, :], x[b].rearrange("(t p) c -> p t c", p=P)).then_inc(xr_in, 16)

            def write_parts(kind, b, c):
                sp.wait_ge(split_done, SPLIT.upto(kind, b, c))
                if kind != "pro":
                    sp.wait_ge(stack_in[c], (b + 1) * 7 * 16)
                sp.dma_start(scr[c].rearrange("s p t -> p s t"), parts[:, :, :]).then_inc(scr_written, 16)

            def read_stack(kind, b, c):
                sp.wait_ge(scr_written, 16 * SPLIT.upto(kind, b, c))
                sp.sem_inc(passed, 1)
                if kind != "pro":
                    sp.wait_ge(scalar_filled, SU.upto(kind, b, ("st", c, NST - 1)))
                rows = scr[c].rearrange("s (d h) t -> (s d) h t", h=HU)
                at = 0
                for n in (3, 2, 1):
                    sp.dma_start(stack[c][at:at + n * D, :, 0:K0], rows[0:n * D, :, 0:K0]).then_inc(stack_in[c], 16)
                    at += n * D
                at = 0
                for first, n in ((0, 2), (0, 2), (0, 1), (2, 1)):
                    sp.dma_start(stack[c][at:at + n * D, :, K0:ALLC],
                                 rows[first * D:(first + n) * D, :, K0:ALLC]).then_inc(stack_in[c], 16)
                    at += n * D

            def max_rows(kind, b, c):
                sp.wait_ge(vector_drained, VU.upto(kind, b, ("mT", c)))
                sp.dma_start(mscr[c].rearrange("s (h t) -> (s h) t", t=T), mT[c][:, :]).then_inc(m_stored, 16)
                sp.wait_ge(m_stored, 16 * MSPLIT.upto(kind, b, c))
                sp.dma_start(stack[c][STACK:STACK + MROWS, :, 0:K0],
                             mscr[c].rearrange("s (h t) -> s h t", h=HU)).then_inc(m_in[c], 16)

            load_x(0)
            load_ctx(0)
            wnat = {"q": W["Wq"], "cq": W["Wcq"], "k": W["Wk"]}
            for n, w in wnat.items():
                sp.dma_start(raw[n], w.rearrange("(k p) c -> p k c", p=P)).then_inc(weights_in, 16)
            sp.dma_start(raw_ck, W["Wck"]).then_inc(weights_in, 16)
            sp.dma_start(wv[:, :, :], W["Wv"].rearrange("(k p) c -> p k c", p=P)).then_inc(weights_in, 16)
            sp.dma_start(wcv[:, :], W["Wcv"]).then_inc(weights_in, 16)
            for i, n in enumerate(("bq", "bcq", "bk", "bck")):
                sp.dma_start(bias_rows[2 * i:2 * i + 2, :], W[n].rearrange("(c p) -> c p", p=P)).then_inc(weights_in, 16)
            for c in range(KC):
                for t in range(QT):
                    sp.dma_start(bv[:, c, t, :], W["bv"][c * P:(c + 1) * P].partition_broadcast(P)).then_inc(weights_in, 16)
            sp.dma_start(bcv[:, :], W["bcv"].partition_broadcast(P)).then_inc(weights_in, 16)
            sp.dma_start(bpg[:, :], W["bp"].partition_broadcast(P)).then_inc(weights_in, 16)
            sp.dma_start(gate[:, :], g_xattn.partition_broadcast(P)).then_inc(weights_in, 16)
            sp.dma_start(wp[:, :, :], W["Wp"].rearrange("(k p) c -> p k c", p=P)).then_inc(weights_in, 16)
            load_xr(0)

            def body(kind, b, two_ahead=True):
                prev, cur, nxt = PARTS[kind]
                if cur:
                    max_rows(kind, b, 0)
                if nxt and two_ahead:
                    sp.wait_ge(xn_ready, LN.upto(kind, b, 0))
                    load_x(1 if kind == "pro" else b + 2)
                    sp.wait_ge(scalar_filled, SU.upto(kind, b, ("xT", QT - 1)))
                    load_ctx(1 if kind == "pro" else b + 2)
                if prev:
                    sp.wait_ge(vector_drained, VU.upto(kind, b, ("wp", QT - 1)))
                    sp.dma_start(x1s[b - 1].rearrange("(t p) c -> p t c", p=P), xr[:, :, :]).then_inc(x1_stored, 16)
                if nxt:
                    write_parts(kind, b, 0)
                    read_stack(kind, b, 0)
                if prev:
                    sp.wait_ge(x1_stored, b * 16)
                    if cur:
                        load_xr(b)
                if cur:
                    max_rows(kind, b, 1)
                if nxt:
                    write_parts(kind, b, 1)
                    read_stack(kind, b, 1)

            body("pro", 0)
            body("first", 0)
            with sp.Fori(1, B - 2) as b:
                body("mid", b)
            body("mid", B - 2, two_ahead=False)
            body("last", B - 1)
            body("post", B)

        @block.gpsimd
        def _(pool):
            pool.memset(half[:, :], -0.5).then_inc(setup_pool, 1)
            pool.memset(ident[:, :], 0.0).then_inc(setup_pool, 1)
            pool.memset(tri[:, :, :], 0.0).then_inc(setup_pool, 1)
            pool.wait_ge(setup_pool, 3)
            pool.affine_select(out=ident[:, :], in_=ident[:, :], compare_op=ALU.not_equal, fill=1.0, base=0,
                               pattern=[[-1, P]], channel_multiplier=1).then_inc(setup_pool, 1)
            pool.affine_select(out=tri[:, :, :], in_=tri[:, :, :], compare_op=ALU.is_ge, fill=-BIG, base=0,
                               pattern=[[0, 4], [-1, P]], channel_multiplier=1).then_inc(setup_pool, 1)
            pool.wait_ge(setup_pool, 5)
            pool.tensor_copy(ident_b[:, :], ident[:, :]).then_inc(setup_pool, 1)
            pool.memset(vst[:, :, :, :, :], 0.0).then_inc(setup_pool, 1)
            pool.memset(vcst[:, :, :, :], 0.0).then_inc(setup_pool, 1)
            for c in range(KC):
                pool.wait_ge(setup_pool, 8 + c)
                pool.memset(stack[c][96:128, :, K0:ALLC], 1.0).then_inc(setup_pool, 1)
            pool.wait_ge(setup_pool, 10)
            pool.memset(vst[:, :, :, :, D:D + 1], 1.0).then_inc(setup_pool, 1)
            pool.memset(vcst[0:TC, :, :, D:D + 1], 1.0).then_inc(setup_pool, 1)
            pool.wait_ge(setup_pool, 12)
            pool.memset(vcst[TC:P, :, :, 32 + D:33 + D], 1.0).then_inc(setup_pool, 1)

            def rstd_of(kind, b):
                n = LN.upto(kind, b, 0)
                pool.wait_ge(mv_ready, n)
                pool.sem_inc(passed, 1)
                pool.tensor_scalar(rstd[:, :], mv[:, :, 1], EPS, None, ALU.add).then_inc(rstd_step, 1)
                pool.wait_ge(rstd_step, n)
                pool.tensor_tensor(rstd[:, :], rstd[:, :], half[:, :], ALU.pow).then_inc(rstd_ready, 1)

            def split_max(kind, b, c):
                n = MSPLIT.upto(kind, b, c)
                pool.wait_ge(vector_drained, VU.start(kind, b) if c == 0 else VU.upto(kind, b, ("sm", 1, NSM - 1)))
                if c == 1:
                    pool.wait_ge(vector_filled, VU.upto(kind, b, ("mT", 0)))
                pool.sem_inc(passed, 1)
                src = nmax[c][:, :, :, :].rearrange("p q h s -> p q (h s)")
                h, m, l = (mparts[:, :, i, :] for i in range(3))
                pool.tensor_copy(h, src).then_inc(msplit_step, 1)
                pool.wait_ge(msplit_step, 3 * n - 2)
                pool.tensor_tensor(mres[:, :, :], src, h, ALU.subtract).then_inc(msplit_step, 1)
                pool.wait_ge(msplit_step, 3 * n - 1)
                pool.sem_inc(passed, 1)
                pool.tensor_copy(m, mres[:, :, :]).then_inc(msplit_step, 1)
                pool.wait_ge(msplit_step, 3 * n)
                pool.tensor_tensor(l, mres[:, :, :], m, ALU.subtract).then_inc(msplit_done, 1)

            def residual_of(kind, b, c, part):
                n = SPLIT.upto(kind, b, c)
                if part == 0:
                    pool.wait_ge(h_ready, n)
                    pool.tensor_tensor(q32[:, :], q32[:, :], parts[:, 0, :], ALU.subtract).then_inc(r_ready, 1)
                else:
                    pool.wait_ge(m_ready, n)
                    pool.tensor_tensor(parts[:, 2, :], q32[:, :], parts[:, 1, :], ALU.subtract).then_inc(split_done, 1)

            def mask_group(kind, b, c, g):
                for k, name in enumerate(GROUP):
                    if name[0] == "X":
                        continue
                    s = PT_SLOT[name]
                    pool.wait_ge(scalar_drained, SU.upto(kind, b, ("st", c, len(GROUP) * g + k)))
                    pool.sem_inc(passed, 1)
                    if name[0] == "A":
                        v, pat = pt[g][:, s, 0:P], [[1, P]]
                    else:
                        step = {"B": 3 * P, "C": 2 * P}[name[0]]
                        v = pt[g][:, s, 0:512].rearrange("p (a k) -> p a k", k=P)[:, 0:4:step // P, :]
                        pat = [[0, 2], [1, P]]
                    pool.affine_select(out=v, in_=v, compare_op=ALU.is_ge, fill=0.0, base=0, pattern=pat,
                                       channel_multiplier=-1).then_inc(masked, 1)

            def add_cross(kind, b, c, g):
                pool.wait_ge(vector_drained, VU.upto(kind, b, ("tU", c, g, "s")))
                h = HU * c + HEAD_GROUP * g
                dst = y[:, :, h:h + HEAD_GROUP, :]
                pool.tensor_tensor(dst, dst, yc[g][:, :, :, :], ALU.add).then_inc(y_added, 1)

            def body(kind, b):
                prev, cur, nxt = PARTS[kind]
                for c in range(KC):
                    if cur:
                        split_max(kind, b, c)
                    if nxt and c == 0:
                        rstd_of(kind, b)
                    if prev and c == 0:
                        add_cross(kind, b, 1, 1)
                        pool.wait_ge(xr_in, b * 16)
                        for t in range(QT):
                            last = pool.tensor_tensor(xr[:, t, :], xr[:, t, :], bpg[:, :], ALU.add)
                        last.then_inc(xres_ready, 1)
                    if cur and c == 1:
                        add_cross(kind, b, 0, 1)
                    if nxt:
                        residual_of(kind, b, c, 0)
                        residual_of(kind, b, c, 1)
                    if cur:
                        mask_group(kind, b, c, 0)
                        mask_group(kind, b, c, 1)
                        add_cross(kind, b, c, 0)

            pool.wait_ge(setup_vec, 7)
            pool.wait_ge(y_added, 4)
            over_batches(pool, body)

        @block.scalar
        def _(act):
            act.wait_ge(weights_in, 16 * NW)
            act.activation(gate[:, :], gate[:, :], ACT.Tanh).then_inc(gate_ready, 1)
            act.wait_ge(setup_vec, 7)

            def bank(kind, name):
                return banks_s[SU.slot(kind, name, RING)]

            def transposed(kind, b):
                for t in range(QT):
                    act.wait_ge(scalar_filled, SU.upto(kind, b, ("xT", t)))
                    ps = bank(kind, ("xT", t))
                    if t == QT - 1:
                        act.activation(ctxT[:, :], ps[:, KC * P:(KC + 1) * P], ACT.Copy)
                    src = ps[:, 0:KC * P].rearrange("p (k t) -> p k t", k=KC)
                    act.activation(xnT[:, :, t * P:(t + 1) * P], src, ACT.Copy).then_inc(scalar_drained, 1)

            def projected(kind, b, c):
                n = SPLIT.upto(kind, b, c)
                if n > 1 if kind == "pro" else True:
                    act.wait_ge(split_done, n - 1)
                for i, (at, w) in enumerate(((Q0, T), (CQ0, T), (K0, T), (KC0, TC))):
                    act.wait_ge(scalar_filled, SU.upto(kind, b, ("proj", c, i)))
                    act.activation(q32[:, at:at + w], bank(kind, ("proj", c, i))[:, 0:w], ACT.Identity,
                                   bias=bias[:, 2 * i + c:2 * i + c + 1]).then_inc(scalar_drained, 1)
                if n > 1 if kind == "pro" else True:
                    act.wait_ge(scr_written, 16 * (n - 1))
                act.wait_ge(scalar_drained, SU.upto(kind, b, ("proj", c, 3)))
                act.activation(parts[:, 0, :], q32[:, :], ACT.Copy).then_inc(h_ready, 1)

            def middle_part(kind, b, c):
                n = SPLIT.upto(kind, b, c)
                act.wait_ge(r_ready, n)
                act.activation(parts[:, 1, :], q32[:, :], ACT.Copy).then_inc(m_ready, 1)

            def unnormalised(kind, b, w, c, g):
                if c == 1:
                    act.wait_ge(vector_filled, VU.upto(kind, b, ("tU", 0, g, w)))
                elif g == 0:
                    act.wait_ge(vector_filled, VU.start(kind, b))
                elif PARTS[kind][0]:
                    act.wait_ge(vector_filled, VU.upto(kind, b, ("tU", 1, 1, w)))
                act.wait_ge(pv_filled, PV.upto(kind, b, (w, c, g)))
                act.activation(usum[w, g][:, :], (pv_cross if w == "x" else pv_self)[:, :], ACT.Copy).then_inc(pv_drained, 1)

            def exponentials(kind, b, c, k):
                g, name = k // len(GROUP), GROUP[k % len(GROUP)]
                if k % len(GROUP) == 0:
                    act.wait_ge(pv_filled, PV.upto(kind, b, ("s", c, g)) - 4)
                act.wait_ge(scalar_filled, SU.upto(kind, b, ("st", c, k)))
                dst = ct[g][:, name[1], :] if name[0] == "X" else pt[g][:, PT_SLOT[name], :]
                act.activation(dst, bank(kind, ("st", c, k))[:, :], ACT.Exp, scale=SCALE).then_inc(scalar_drained, 1)

            def body(kind, b):
                prev, cur, nxt = PARTS[kind]
                for c in range(KC):
                    if nxt and c == 0:
                        transposed(kind, b)
                    if nxt:
                        projected(kind, b, c)
                    if cur:
                        for k in range(NST):
                            exponentials(kind, b, c, k)
                            if k == 5 and nxt:
                                middle_part(kind, b, c)
                            if k == 18:
                                unnormalised(kind, b, "x", c, 0)
                        unnormalised(kind, b, "s", c, 0)
                        unnormalised(kind, b, "x", c, 1)
                        unnormalised(kind, b, "s", c, 1)
                    elif nxt:
                        middle_part(kind, b, c)

            over_batches(act, body)

        @block.vector
        def _(dve):
            dve.wait_ge(weights_in, 16 * NW)
            for i, n in enumerate(("q", "cq", "k")):
                dve.tensor_copy(wq[n][:, :, :, :].rearrange("p k c (d h) -> p (k c) d h", h=HU),
                                raw[n].rearrange("p k (c h d) -> p (k c) d h", c=KC, d=D)).then_inc(setup_vec, 1)
            dve.tensor_copy(wck[:, :, :].rearrange("p c (d h) -> p c d h", h=HU),
                            raw_ck.rearrange("p (c h d) -> p c d h", c=KC, d=D)).then_inc(setup_vec, 1)
            dve.tensor_copy(bias_perm[:, :].rearrange("r (d h) -> r d h", h=HU),
                            bias_rows[:, :].rearrange("r (h d) -> r d h", d=D)).then_inc(setup_vec, 1)
            dve.wait_ge(gate_ready, 1)
            dve.tensor_scalar(wp[:, :, :], wp[:, :, :], gate[:, 0:1], None, ALU.mult).then_inc(setup_vec, 1)
            dve.tensor_scalar(bpg[:, :], bpg[:, :], gate[:, 0:1], None, ALU.mult).then_inc(y_added, 4)
            dve.wait_ge(setup_pe, 1)
            dve.tensor_copy(bias[:, :], banks_v[0][:, 0:8]).then_inc(setup_vec, 1)
            dve.memset(recip["x"][:, :, :], 1.0).then_inc(pv_filled, 8)
            dve.memset(mres[:, :, :], 0.0).then_inc(pv_drained, 8)
            dve.wait_ge(pv_filled, 8)
            dve.wait_ge(setup_pool, 13)

            def bank(kind, name):
                return banks_v[VU.slot(kind, name, RING)]

            def filled(kind, b, name):
                dve.wait_ge(vector_filled, VU.upto(kind, b, name))
                return bank(kind, name)

            def ln_stats(kind, b):
                n = LN.upto(kind, b, 0)
                dve.wait_ge(x_in, 16 * n)
                for t in range(QT):
                    last = dve.bn_stats(stats[:, t, :], xt[:, t, :])
                last.then_inc(stats_ready, 1)
                dve.wait_ge(stats_ready, n)
                dve.sem_inc(passed, 1)
                for t in range(QT):
                    last = dve.bn_aggr(mv[:, t, :], stats[:, t, :])
                last.then_inc(mv_ready, 1)

            def ln_apply(kind, b):
                dve.wait_ge(rstd_ready, LN.upto(kind, b, 0))
                if kind != "pro":
                    dve.wait_ge(scalar_filled, SU.start(kind, b))
                for t in range(QT):
                    last = dve.tensor_scalar(xn[:, t, :], xt[:, t, :], mv[:, t, 0:1], rstd[:, t:t + 1],
                                             ALU.subtract, ALU.mult)
                last.then_inc(xn_ready, 1)

            def values(kind, b, c):
                if kind != "pro":
                    dve.wait_ge(pv_filled, PV.start(kind, b) if c == 1 else PV.upto(kind, b, ("s", 0, 1)))
                ps = filled(kind, b, ("v", c))
                dve.tensor_tensor(vst[:, :, c, :, 0:D], ps[:, :].rearrange("p (t h d) -> p t h d", t=QT, d=D),
                                  bv[:, c, :, :].rearrange("p t (h d) -> p t h d", d=D), ALU.add).then_inc(vector_drained, 1)
                ps = filled(kind, b, ("vc", c))
                for half_, col in ((0, 0), (1, 32)):
                    rows = slice(half_ * TC, (half_ + 1) * TC)
                    last = dve.tensor_tensor(
                        vcst[rows, c, :, col:col + D],
                        ps[rows, 0:P].rearrange("p (a i d) -> p a i d", i=2, d=D)[:, :, half_, :],
                        bcv[rows, c * P:(c + 1) * P].rearrange("p (a i d) -> p a i d", i=2, d=D)[:, :, half_, :], ALU.add)
                last.then_inc(vector_drained, 1)

            def maxima(kind, b, c, ks):
                for k in ks:
                    what, qt, h, n = MAXU[k]
                    ps = filled(kind, b, ("sm", c, k))
                    if what == "cross":
                        src, dst = ps[:, :].rearrange("p (h t) -> p h t", t=TC), nmax[c][:, qt, :, 1]
                    else:
                        w = (qt + 1) * P
                        src = ps[:, 0:n * w].rearrange("p (h t) -> p h t", t=w)
                        dst = nmax[c][:, qt, h:h + n, 0]
                    dve.tensor_reduce(dst, src, axis=AX, op=ALU.max, negate=True).then_inc(vector_drained, 1)

            def max_transposed(kind, b, c):
                ps = filled(kind, b, ("mT", c))
                dve.tensor_copy(mT[c][:, :], ps[:, :].bitcast(BF16)[0:3 * HU * 2, 0:T]).then_inc(vector_drained, 1)

            def normalise(kind, b, c, g):
                n = 2 * YADD.upto(kind, b, (c, g)) - 2 * YADD.credit
                h = HU * c + HEAD_GROUP * g
                for w, dst in (("x", yc[g][:, :, :, :]), ("s", y[:, :, h:h + HEAD_GROUP, :])):
                    if w == "x":
                        dve.wait_ge(y_added, YADD.upto(kind, b, (c, g)) - 2)
                    ps = filled(kind, b, ("tU", c, g, w))[:, :].rearrange("p (t j r) -> p t j r", t=QT, r=32)
                    dve.reciprocal(recip[w][:, :, :], ps[:, :, :, D]).then_inc(norm_step, 1)
                    dve.wait_ge(norm_step, n - 1 if w == "x" else n)
                    dve.tensor_tensor(dst, ps[:, :, :, 0:D], recip[w][:, :, :].unsqueeze(3).to_broadcast([P, QT, HEAD_GROUP, D]),
                                      ALU.mult).then_inc(vector_drained, 1)

            def output_rows(kind, b):
                for k in range(KC):
                    ps = filled(kind, b, ("yT", k))
                    dve.tensor_copy(yT[:, k, :], ps[:, :]).then_inc(vector_drained, 1)
                dve.wait_ge(xres_ready, b)
                for t in range(QT):
                    ps = filled(kind, b, ("wp", t))
                    dve.tensor_tensor(xr[:, t, :], ps[:, 0:C], xr[:, t, :], ALU.add).then_inc(vector_drained, 1)

            def body(kind, b):
                prev, cur, nxt = PARTS[kind]
                if nxt:
                    ln_stats(kind, b)
                if cur:
                    values(kind, b, 1)
                if prev:
                    normalise(kind, b, 1, 1)
                if nxt:
                    ln_apply(kind, b)
                if cur:
                    max_transposed(kind, b, 0)
                if prev:
                    output_rows(kind, b)
                for c in range(KC):
                    other = 1 - c
                    if c == 1:
                        if nxt:
                            values(kind, b, 0)
                        if cur:
                            normalise(kind, b, 0, 1)
                            max_transposed(kind, b, 1)
                    work = cur if c == 0 else nxt
                    if work:
                        maxima(kind, b, other, range(SM_MID))
                    if cur:
                        normalise(kind, b, c, 0)
                    if work:
                        maxima(kind, b, other, range(SM_MID, NSM))

            over_batches(dve, body)

        @block.tensor
        def _(pe):
            pe.wait_ge(setup_pool, 13)
            pe.wait_ge(setup_vec, 5)
            pe.transpose(banks_v[0][:, 0:8], bias_perm[:, :], ident[0:8, 0:8]).then_inc(setup_pe, 1)
            pe.wait_ge(setup_vec, 7)
            pe.wait_ge(y_added, 4)

            def claim_s(kind, b, name):
                n = SU.upto(kind, b, name) - RING
                if kind != "pro" or n > 0:
                    pe.wait_ge(scalar_drained, n)
                return banks_s[SU.slot(kind, name, RING)]

            def claim_v(kind, b, name):
                n = VU.upto(kind, b, name) - RING
                if kind != "pro" or n > 0:
                    pe.wait_ge(vector_drained, n)
                return banks_v[VU.slot(kind, name, RING)]

            def value_products(kind, b, c):
                ps = claim_v(kind, b, ("v", c))
                for t in range(QT):
                    for k in range(KC):
                        last = pe.matmul(ps[:, t * P:(t + 1) * P], xnT[:, k, t * P:(t + 1) * P],
                                         wv[:, k, c * P:(c + 1) * P], start=(k == 0), stop=(k == KC - 1))
                last.then_inc(vector_filled, 1)
                ps = claim_v(kind, b, ("vc", c))
                pe.matmul(ps[:, 0:P], ctxT[:, :], wcv[:, c * P:(c + 1) * P], start=True, stop=True).then_inc(vector_filled, 1)

            def transpose_max(kind, b, c):
                ps = claim_v(kind, b, ("mT", c))
                pe.wait_ge(msplit_done, MSPLIT.upto(kind, b, c))
                pe.sem_inc(passed, 1)
                for q in range(QT):
                    last = pe.transpose(ps[:, :].bitcast(BF16)[0:3 * HU * 2, q * P:(q + 1) * P],
                                        mparts[:, q, :, :].rearrange("p s h -> p (s h)"), ident_b[:, :])
                last.then_inc(vector_filled, 1)

            def transpose_inputs(kind, b):
                pe.wait_ge(xn_ready, LN.upto(kind, b, 0))
                pe.wait_ge(ctx_in, 32 * LN.upto(kind, b, 0))
                for t in range(QT):
                    ps = claim_s(kind, b, ("xT", t))
                    if t == QT - 1:
                        pe.transpose(ps[:, KC * P:(KC + 1) * P], ctile[:, :], ident[:, :])
                    for k in range(KC):
                        last = pe.transpose(ps[:, k * P:(k + 1) * P], xn[:, t, k * P:(k + 1) * P], ident[:, :])
                    last.then_inc(scalar_filled, 1)
                pe.wait_ge(scalar_drained, SU.upto(kind, b, ("xT", QT - 1)))

            def transpose_sums(kind, b, c, g):
                for w in ("x", "s"):
                    ps = claim_v(kind, b, ("tU", c, g, w))
                    pe.wait_ge(pv_drained, PV.upto(kind, b, (w, c, g)) if PARTS[kind][1] and not (c, g) == (1, 1)
                               else PV.start(kind, b))
                    for t in range(QT):
                        last = pe.transpose(ps[:, t * P:(t + 1) * P], usum[w, g][:, t * P:(t + 1) * P], ident[:, :])
                    last.then_inc(vector_filled, 1)

            def projections(kind, b, c, which):
                for i in which:
                    ps = claim_s(kind, b, ("proj", c, i))
                    if i == 3:
                        pe.matmul(ps[:, 0:TC], wck[:, c, :], ctxT[:, 0:TC], start=True, stop=True).then_inc(scalar_filled, 1)
                        continue
                    for k in range(KC):
                        last = pe.matmul(ps[:, :], wq[("q", "cq", "k")[i]][:, k, c, :], xnT[:, k, :],
                                         start=(k == 0), stop=(k == KC - 1))
                    last.then_inc(scalar_filled, 1)

            def score_unit(kind, b, c, k):
                g, (what, j) = k // len(GROUP), GROUP[k % len(GROUP)]
                ps = claim_s(kind, b, ("st", c, k))
                rows = STACK + MROWS

                def mm(out, head, key0, nk, q0, nq, **kw):
                    return pe.matmul(out, stack[c][0:rows, head, key0:key0 + nk], stack[c][0:rows, head, q0:q0 + nq],
                                     start=True, stop=True, **kw)

                h = HEAD_GROUP * g + j
                if what == "X":
                    h = HEAD_GROUP * g + 2 * j
                    for i in range(2):
                        last = mm(ps[i * TC:(i + 1) * TC, :], h + i, KC0, TC, CQ0, T)
                elif what == "A":
                    last = mm(ps[:, :], h, K0, P, Q0, T)
                elif what == "B":
                    mm(ps[:, 0:3 * P], h, K0 + P, P, Q0 + P, 3 * P)
                    last = mm(ps[:, 3 * P:], h, K0 + 3 * P, P, Q0 + 3 * P, P)
                else:
                    for i in range(2):
                        last = mm(ps[:, i * 2 * P:(i + 1) * 2 * P], h + i, K0 + 2 * P, P, Q0 + 2 * P, 2 * P)
                last.then_inc(scalar_filled, 1)

            def max_unit(kind, b, c, k):
                what, qt, h0, n = MAXU[k]
                ps = claim_v(kind, b, ("sm", c, k))
                if what == "cross":
                    for h in range(n):
                        last = pe.matmul(ps[:, h * TC:(h + 1) * TC], stack[c][0:STACK, h, CQ0 + qt * P:CQ0 + (qt + 1) * P],
                                         stack[c][0:STACK, h, KC0:KC0 + TC], start=True, stop=True)
                else:
                    w = (qt + 1) * P
                    pe.matmul(ps[:, 0:n * w].rearrange("p (h t) -> p h t", t=w)[:, :, qt * P:w], ident_b[:, :],
                              tri[:, 0:n, :], start=True, stop=False, skip_group_check=True)
                    for i in range(n):
                        last = pe.matmul(ps[:, i * w:(i + 1) * w], stack[c][0:STACK, h0 + i, qt * P:(qt + 1) * P],
                                         stack[c][0:STACK, h0 + i, K0:K0 + w], start=False, stop=(i == n - 1),
                                         skip_group_check=True)
                last.then_inc(vector_filled, 1)

            def pv_cross_products(kind, b, c, g):
                pe.wait_ge(pv_drained, PV.upto(kind, b, ("x", c, g)) - 2)
                pe.wait_ge(scalar_drained, SU.upto(kind, b, ("st", c, len(GROUP) * g + 1)))
                for jp in range(2):
                    last = pe.matmul(pv_cross[64 * jp:64 * jp + 64, :], vcst[:, c, 2 * g + jp, :], ct[g][:, jp, :],
                                     start=True, stop=True)
                last.then_inc(pv_filled, 1)

            def pv_self_products(kind, b, c, g, kt):
                if kt == 0:
                    pe.wait_ge(pv_drained, PV.upto(kind, b, ("s", c, g)) - 2)
                    pe.wait_ge(masked, MASKED.upto(kind, b, (c, g, 9)))
                for j in range(4):
                    if kt == 0:
                        src = pt[g][:, PT_SLOT[("A", j)], :]
                    elif kt == 1:
                        src = pt[g][:, PT_SLOT[("B", j)], 0:3 * P]
                    elif kt == 3:
                        src = pt[g][:, PT_SLOT[("B", j)], 3 * P:]
                    else:
                        src = pt[g][:, PT_SLOT[("C", j // 2 * 2)], (j % 2) * 2 * P:(j % 2 + 1) * 2 * P]
                    last = pe.matmul(pv_self[32 * j:32 * j + 32, kt * P:T], vst[:, kt, c, HEAD_GROUP * g + j, :], src,
                                     start=(kt == 0), stop=(kt == QT - 1), skip_group_check=True)
                if kt == QT - 1:
                    last.then_inc(pv_filled, 1)

            def main(kind, b, c):
                prev, cur, nxt = PARTS[kind]
                work = cur if c == 0 else nxt
                other = 1 - c
                if work:
                    pe.wait_ge(stack_in[other], 16 * 7 * (b + 1 if c == 0 else LN.upto(kind, b, 0)))
                if cur:
                    pe.wait_ge(m_in[c], 16 * (b + 1))
                    pe.wait_ge(vector_drained, VU.start(kind, b))
                for k in range(NST):
                    if cur:
                        score_unit(kind, b, c, k)
                        if k == 14:
                            pv_cross_products(kind, b, c, 0)
                        if k in (16, 18, 20, 22):
                            pv_self_products(kind, b, c, 0, (k - 16) // 2)
                    if work and k < SM_LOOP:
                        max_unit(kind, b, other, k)
                if work:
                    for k in range(SM_LOOP, SM_MID):
                        max_unit(kind, b, other, k)
                if cur:
                    pv_cross_products(kind, b, c, 1)
                    for kt in range(QT):
                        pv_self_products(kind, b, c, 1, kt)
                    transpose_sums(kind, b, c, 0)
                if work:
                    for k in range(SM_MID, NSM):
                        max_unit(kind, b, other, k)

            def transpose_output(kind, b):
                pe.wait_ge(y_added, YADD.upto(kind, b, (1, 1)))
                for k in range(KC):
                    ps = claim_v(kind, b, ("yT", k))
                    for t in range(QT):
                        last = pe.transpose(ps[:, t * P:(t + 1) * P],
                                            y[:, t, HU * k:HU * (k + 1), :].rearrange("p h d -> p (h d)"), ident[:, :])
                    last.then_inc(vector_filled, 1)

            def output_projection(kind, b):
                pe.wait_ge(vector_drained, VU.upto(kind, b, ("yT", KC - 1)))
                for t in range(QT):
                    ps = claim_v(kind, b, ("wp", t))
                    for k in range(KC):
                        last = pe.matmul(ps[:, 0:C], yT[:, k, t * P:(t + 1) * P], wp[:, k, :], start=(k == 0),
                                         stop=(k == KC - 1))
                    last.then_inc(vector_filled, 1)

            def body(kind, b):
                prev, cur, nxt = PARTS[kind]
                if cur:
                    value_products(kind, b, 1)
                if prev:
                    transpose_sums(kind, b, 1, 1)
                if cur:
                    transpose_max(kind, b, 0)
                if nxt:
                    transpose_inputs(kind, b)
                    projections(kind, b, 0, (0,))
                if prev:
                    transpose_output(kind, b)
                if nxt:
                    projections(kind, b, 0, (1, 2, 3))
                if prev:
                    output_projection(kind, b)
                main(kind, b, 0)
                if nxt:
                    value_products(kind, b, 0)
                if cur:
                    transpose_sums(kind, b, 0, 1)
                    transpose_max(kind, b, 1)
                if nxt:
                    projections(kind, b, 1, (0, 1, 2, 3))
                main(kind, b, 1)

            over_batches(pe, body)


def routing_phase(nc, x1s, g_ffn, W, sc, keep):
    B, T, C = x1s.shape
    E = W["router_w"].shape[1]
    N = B * T
    QT, KC = T // P, C // P
    I = W["shared_up_w"].shape[1]
    TAPS = W["conv_w"].shape[2]
    PAD = TAPS - 1
    xn_rows, acc, lists = sc["xn_rows"], sc["acc"], sc["lists"]
    NFILL = lists.shape[0] // P

    with ExitStack() as st:
        def sb(name, shape, dt=F32):
            return st.enter_context(nc.sbuf_tensor(name, shape, dt))

        def ps(name):
            return st.enter_context(nc.psum_tensor(name, [P, 512], F32))

        def sem(name):
            return st.enter_context(nc.semaphore(name))

        passed = sem("passed_routing")
        psT = [ps(f"psT{k}") for k in range(KC)]
        psR, psRank, psG, psU = ps("psR"), ps("psRank"), ps("psG"), ps("psU")
        psD = [ps(f"psD{i}") for i in range(2)]

        x1t = [sb(f"x1t{i}", [P, QT, C]) for i in range(2)]
        xn = [sb(f"xn2_{i}", [P, QT, C]) for i in range(2)]
        xT = sb("xT2", [P, KC, PAD + T])
        stats, mv = sb("stats2", [P, QT, 6]), sb("mv2", [P, QT, 2])
        rstd, half = sb("rstd2", [P, QT]), sb("half2", [P, QT])
        conv_raw = sb("conv_raw", [P, C, TAPS])
        conv = sb("conv", [P, KC, TAPS, I])
        up = sb("shared_up", [P, KC, I])
        down = sb("shared_down", [P, C])
        wr = sb("router_w", [P, KC, E])
        rb = sb("router_b", [P, QT, E])
        gate = sb("gate2", [P, 1])
        ident = sb("ident2", [P, P])
        before, ones = sb("before", [P, P], BF16), sb("ones", [P, P], BF16)
        zeros = sb("zeros", [P, NFILL], I32)
        iota_i, iota = sb("iota_i", [P, QT, E], I32), sb("iota", [P, QT, E])
        tok_i, tok = sb("tok_i", [P, QT], I32), sb("tok", [P, QT])
        logit, prob = sb("logit", [P, QT, E]), sb("prob", [P, QT, E])
        m4, z4, s4 = sb("m4", [P, QT]), sb("z4", [P, QT]), sb("s4", [P, QT])
        top, topi = sb("top", [P, QT, 8]), sb("topi", [P, QT, 8], U32)
        topf, w2, wid2 = sb("topf", [P, QT, 2]), sb("w2", [P, QT, 2]), sb("wid2", [P, QT, 2])
        wid = sb("wid", [P, QT])
        hot = [sb(f"hot{k}", [P, QT, E]) for k in range(2)]
        both = sb("both", [P, QT, E], BF16)
        place = sb("place", [P, QT, E])
        sel = sb("sel", [P, QT, E])
        slotf = sb("slotf", [P, 2, QT])
        slot = sb("slot", [P, 2 * QT], U32)
        tokens = sb("tokens", [P, QT], I32)
        th, h = sb("th", [P, T]), sb("hsh", [P, T])
        part = sb("part", [P, QT, C])
        running = sb("running", [P, E])
        run0 = sb("run0", [P, E])

        loaded = sem("b_loaded")
        pool_setup, vec_setup, pe_setup = sem("b_pool_setup"), sem("b_vec_setup"), sem("b_pe_setup")
        gate_ready = sem("b_gate_ready")
        filled_lists = sem("lists_zeroed")
        x1_in = [sem(f"x1_in{i}") for i in range(2)]
        stats_ready, mv_ready, rstd_step, rstd_ready = sem("b_stats"), sem("b_mv"), sem("b_rstd_step"), sem("b_rstd")
        xn_ready = sem("b_xn_ready")
        xn_saved = [sem(f"xn_saved{i}") for i in range(2)]
        xT_filled, xT_drained = sem("xT_filled"), sem("xT_drained")
        router_filled, router_drained = sem("router_filled"), sem("router_drained")
        shifted, exped = sem("logits_shifted"), sem("logits_exp")
        step = sem("route_step")
        hot_ready, rank_filled, slot_ready = sem("hot_ready"), sem("rank_filled"), sem("slot_ready")
        scattered = sem("scattered")
        gu_filled, tanh_ready, h_ready = sem("gu_filled"), sem("tanh_ready"), sem("h_ready_b")
        g_ready = sem("silu_gate_ready")
        part_ready = sem("part_ready")
        down_filled, down_drained = sem("down_filled"), sem("down_drained")
        acc_saved = sem("acc_saved")
        NL = 9

        block = st.enter_context(nc.Block())

        def over_batches(eng, body):
            body("pro", 0, 0)
            body("first", 0, 0)
            with eng.Fori(0, (B - 2) // 2) as i:
                body("mid", 2 * i + 1, 1)
                body("mid", 2 * i + 2, 0)
            body("last", B - 1, 1)

        def flags(kind):
            return kind != "pro", kind != "last"

        def after(kind, b):
            return 0 if kind == "pro" else b + 1

        @block.sync
        def _(sp):
            def load(b, par):
                sp.dma_start(x1t[par][:, :, :], x1s[b].rearrange("(t p) c -> p t c", p=P)).then_inc(x1_in[par], 16)

            load(0, 0)
            load(1, 1)
            sp.dma_start(conv_raw[:, :, :], W["conv_w"]).then_inc(loaded, 16)
            sp.dma_start(up[:, :, :], W["shared_up_w"].rearrange("(k p) i -> p k i", p=P)).then_inc(loaded, 16)
            sp.dma_start(down[:, :], W["shared_down_w"]).then_inc(loaded, 16)
            sp.dma_start(wr[:, :, :], W["router_w"].rearrange("(k p) e -> p k e", p=P)).then_inc(loaded, 16)
            for t in range(QT):
                sp.dma_start(rb[:, t, :], W["router_bias"].partition_broadcast(P)).then_inc(loaded, 16)
            sp.dma_start(gate[:, :], g_ffn.partition_broadcast(P)).then_inc(loaded, 16)
            sp.wait_ge(vec_setup, 1)
            sp.dma_start(lists.rearrange("(p n) a -> p (n a)", p=P), zeros[:, :]).then_inc(filled_lists, 16)

            def body(kind, b, par, two_ahead=True):
                cur, nxt = flags(kind)
                n = after(kind, b)
                if nxt:
                    q = 1 - par if cur else 0
                    sp.wait_ge(xn_ready, n + 1)
                    sp.dma_start(xn_rows.rearrange("(b t p) c -> b p t c", p=P, t=QT)[n], xn[q][:, :, :]).then_inc(xn_saved[q], 16)
                if cur:
                    if two_ahead:
                        sp.wait_ge(part_ready, b + 1)
                        load(b + 2, par)
                    sp.wait_ge(down_drained, 2 * (b + 1))
                    sp.dma_start(acc[b].rearrange("(t p) c -> p t c", p=P), part[:, :, :]).then_inc(acc_saved, 16)

            body("pro", 0, 0)
            body("first", 0, 0)
            with sp.Fori(0, (B - 4) // 2) as i:
                body("mid", 2 * i + 1, 1)
                body("mid", 2 * i + 2, 0)
            body("mid", B - 3, 1)
            body("mid", B - 2, 0, two_ahead=False)
            body("last", B - 1, 1, two_ahead=False)
            sp.wait_ge(acc_saved, 16 * B)
            for i in range(2):
                sp.wait_ge(xn_saved[i], 16 * B // 2)

        @block.gpsimd
        def _(pool):
            pool.memset(ident[:, :], 0.0).then_inc(pool_setup, 1)
            pool.memset(before[:, :], 1.0).then_inc(pool_setup, 1)
            pool.memset(ones[:, :], 1.0).then_inc(pool_setup, 1)
            pool.memset(half[:, :], -0.5).then_inc(pool_setup, 1)
            pool.memset(xT[:, :, 0:PAD], 0.0).then_inc(pool_setup, 1)
            pool.iota(iota_i[:, :, :], pattern=[[0, QT], [1, E]], base=0, channel_multiplier=0).then_inc(pool_setup, 1)
            pool.iota(tok_i[:, :], pattern=[[P, QT]], base=0, channel_multiplier=1).then_inc(pool_setup, 1)
            pool.iota(run0[:, :], pattern=[[N, E]], base=0, channel_multiplier=0,
                      allow_small_or_imprecise_dtypes=True).then_inc(pool_setup, 1)
            pool.wait_ge(pool_setup, 8)
            pool.affine_select(out=ident[:, :], in_=ident[:, :], compare_op=ALU.not_equal, fill=1.0, base=0,
                               pattern=[[-1, P]], channel_multiplier=1).then_inc(pool_setup, 1)
            pool.affine_select(out=before[:, :], in_=before[:, :], compare_op=ALU.is_gt, fill=0.0, base=0,
                               pattern=[[1, P]], channel_multiplier=-1).then_inc(pool_setup, 1)
            pool.wait_ge(filled_lists, 16)

            def body(kind, b, par):
                cur, nxt = flags(kind)
                n = after(kind, b)
                if nxt:
                    pool.wait_ge(mv_ready, n + 1)
                    pool.sem_inc(passed, 1)
                    pool.tensor_scalar(rstd[:, :], mv[:, :, 1], EPS, None, ALU.add).then_inc(rstd_step, 1)
                    pool.wait_ge(rstd_step, n + 1)
                    pool.tensor_tensor(rstd[:, :], rstd[:, :], half[:, :], ALU.pow).then_inc(rstd_ready, 1)
                if cur:
                    pool.wait_ge(slot_ready, b + 1)
                    pool.sem_inc(passed, 1)
                    for k in range(2):
                        for t in range(QT):
                            i = k * QT + t
                            pool.indirect_dma_start(
                                out=lists[:, :], out_offset=bass.IndirectOffsetOnAxis(ap=slot[:, i:i + 1], axis=0),
                                in_=tokens[:, t:t + 1], in_offset=None).then_inc(scattered, 16)

            over_batches(pool, body)
            pool.wait_ge(scattered, 16 * 2 * QT * B)

        @block.scalar
        def _(act):
            act.wait_ge(loaded, 16 * NL)
            act.activation(gate[:, :], gate[:, :], ACT.Tanh).then_inc(gate_ready, 1)

            def body(kind, b, par):
                cur, nxt = flags(kind)
                n = after(kind, b)
                if cur:
                    act.wait_ge(shifted, b + 1)
                    act.activation(prob[:, :, :], logit[:, :, :], ACT.Exp).then_inc(exped, 1)
                    act.wait_ge(gu_filled, b + 1)
                    if kind != "first":
                        act.wait_ge(h_ready, b)
                    act.activation(th[:, :], psG[:, :], ACT.Tanh, scale=0.5).then_inc(tanh_ready, 1)
                if nxt:
                    for k in range(KC):
                        act.wait_ge(xT_filled, 2 * n + k + 1)
                        act.activation(xT[:, k, PAD:], psT[k][:, :], ACT.Copy).then_inc(xT_drained, 1)

            over_batches(act, body)

        @block.vector
        def _(dve):
            steps = [0]
            base = [0]

            def link(ins, per=None):
                steps[0] += 1
                ins.then_inc(step, 1)
                dve.wait_ge(step, base[0] + steps[0])

            dve.memset(zeros[:, :], 0).then_inc(vec_setup, 1)
            dve.wait_ge(pool_setup, 10)
            dve.tensor_copy(iota[:, :, :], iota_i[:, :, :]).then_inc(vec_setup, 1)
            dve.tensor_copy(tok[:, :], tok_i[:, :]).then_inc(vec_setup, 1)
            dve.tensor_copy(running[:, :], run0[:, :]).then_inc(vec_setup, 1)
            dve.wait_ge(gate_ready, 1)
            dve.tensor_scalar(down[:, :], down[:, :], gate[:, 0:1], 0.5, ALU.mult, ALU.mult).then_inc(vec_setup, 1)
            dve.wait_ge(pe_setup, 1)
            for k in range(KC):
                dve.tensor_copy(conv[:, k, :, :].rearrange("p a i -> p (a i)"), psT[k][:, 0:TAPS * I]).then_inc(vec_setup, 1)
            dve.wait_ge(vec_setup, 5 + KC)

            CHAIN = 17

            def body(kind, b, par):
                cur, nxt = flags(kind)
                n = after(kind, b)
                steps[0] = 0
                base[0] = 0 if kind == "pro" else b * CHAIN
                if nxt:
                    q = 1 - par if cur else 0
                    dve.wait_ge(x1_in[q], 8 * (n - q) + 16)
                    for t in range(QT):
                        last = dve.bn_stats(stats[:, t, :], x1t[q][:, t, :])
                    last.then_inc(stats_ready, 1)
                    dve.wait_ge(stats_ready, n + 1)
                    dve.sem_inc(passed, 1)
                    for t in range(QT):
                        last = dve.bn_aggr(mv[:, t, :], stats[:, t, :])
                    last.then_inc(mv_ready, 1)
                if cur:
                    bc = [P, QT, E]
                    dve.wait_ge(router_filled, b + 1)
                    link(dve.tensor_tensor(logit[:, :, :], psR[:, 0:QT * E].rearrange("p (t e) -> p t e", e=E),
                                           rb[:, :, :], ALU.add))
                    link(dve.tensor_reduce(m4[:, :], logit[:, :, :], axis=AX, op=ALU.max))
                    dve.tensor_tensor(logit[:, :, :], logit[:, :, :], m4[:, :].unsqueeze(2).to_broadcast(bc),
                                      ALU.subtract).then_inc(shifted, 1)
                    dve.wait_ge(exped, b + 1)
                    link(dve.tensor_reduce(z4[:, :], prob[:, :, :], axis=AX, op=ALU.add))
                    link(dve.reciprocal(z4[:, :], z4[:, :]))
                    link(dve.tensor_tensor(prob[:, :, :], prob[:, :, :], z4[:, :].unsqueeze(2).to_broadcast(bc), ALU.mult))
                    dve.sem_inc(passed, 1)
                    for t in range(QT):
                        last = dve.max(top[:, t, :], prob[:, t, :])
                    link(last)
                    dve.sem_inc(passed, 1)
                    for t in range(QT):
                        last = dve.max_index(topi[:, t, :], top[:, t, :], prob[:, t, :])
                    link(last)
                    dve.tensor_tensor(s4[:, :], top[:, :, 0], top[:, :, 1], ALU.add)
                    link(dve.tensor_copy(topf[:, :, :], topi[:, :, 0:2]))
                    dve.tensor_scalar(s4[:, :], s4[:, :], 1e-6, None, ALU.add)
                    for k in range(2):
                        last = dve.tensor_tensor(hot[k][:, :, :], iota[:, :, :], topf[:, :, k].unsqueeze(2).to_broadcast(bc),
                                                 ALU.is_equal)
                    link(last)
                    dve.tensor_tensor(both[:, :, :], hot[0][:, :, :], hot[1][:, :, :], ALU.add).then_inc(hot_ready, 1)
                    link(dve.reciprocal(s4[:, :], s4[:, :]))
                    dve.tensor_scalar(wid2[:, :, :], topf[:, :, :], float(E - 1), gate[:, 0:1], ALU.is_equal, ALU.mult)
                    link(dve.tensor_tensor(w2[:, :, :], top[:, :, 0:2], s4[:, :].unsqueeze(2).to_broadcast([P, QT, 2]), ALU.mult))
                    link(dve.tensor_tensor(wid2[:, :, :], w2[:, :, :], wid2[:, :, :], ALU.mult))
                    link(dve.tensor_reduce(wid[:, :], wid2[:, :, :], axis=AX, op=ALU.add))
                    link(dve.scalar_tensor_tensor(out=keep["weight"][:, bass.ds(b * QT, QT), :], in0=w2[:, :, :],
                                                  scalar=gate[:, 0:1], in1=wid2[:, :, :], op0=ALU.mult, op1=ALU.subtract))
                    if kind != "first":
                        dve.wait_ge(acc_saved, 16 * b)
                    for t in range(QT):
                        last = dve.scalar_tensor_tensor(out=part[:, t, :], in0=xn[par][:, t, :], scalar=wid[:, t:t + 1],
                                                        in1=x1t[par][:, t, :], op0=ALU.mult, op1=ALU.add)
                    last.then_inc(part_ready, 1)
                if nxt:
                    dve.wait_ge(rstd_ready, n + 1)
                    if kind not in ("pro", "first"):
                        dve.wait_ge(xn_saved[q], 8 * (n - q))
                    for t in range(QT):
                        last = dve.tensor_scalar(xn[q][:, t, :], x1t[q][:, t, :], mv[:, t, 0:1], rstd[:, t:t + 1],
                                                 ALU.subtract, ALU.mult)
                    last.then_inc(xn_ready, 1)
                if cur:
                    dve.wait_ge(tanh_ready, b + 1)
                    dve.scalar_tensor_tensor(out=h[:, :], in0=th[:, :], scalar=1.0, in1=psG[:, :],
                                             op0=ALU.add, op1=ALU.mult).then_inc(g_ready, 1)
                    dve.wait_ge(g_ready, b + 1)
                    dve.tensor_tensor(h[:, :], h[:, :], psU[:, :], ALU.mult).then_inc(h_ready, 1)
                    dve.wait_ge(rank_filled, b + 1)
                    link(dve.tensor_tensor(place[:, :, :], psRank[:, 0:QT * E].rearrange("p (t e) -> p t e", e=E),
                                           running[:, :].unsqueeze(1).to_broadcast(bc), ALU.add))
                    if kind != "first":
                        dve.wait_ge(scattered, 16 * 2 * QT * b)
                    dve.tensor_tensor(running[:, :], running[:, :], psRank[:, QT * E:(QT + 1) * E], ALU.add)
                    for k in range(2):
                        dve.tensor_tensor(hot[k][:, :, :], hot[k][:, :, :], place[:, :, :], ALU.mult).then_inc(step, 1)
                    dve.wait_ge(step, b * CHAIN + CHAIN)
                    for k in range(2):
                        last = dve.tensor_reduce(slotf[:, k, :], hot[k][:, :, :], axis=AX, op=ALU.add)
                    last.then_inc(keep["step"], 1)
                    dve.wait_ge(keep["step"], b + 1)
                    dve.tensor_copy(tokens[:, :], tok[:, :])
                    dve.tensor_scalar(tok[:, :], tok[:, :], float(T), None, ALU.add)
                    dve.tensor_copy(keep["row"][:, bass.ds(b * 2, 2), :], slotf[:, :, :])
                    dve.tensor_copy(slot[:, :], slotf[:, :, :].rearrange("p k t -> p (k t)")).then_inc(slot_ready, 1)
                    for i in range(2):
                        dve.wait_ge(down_filled, 2 * b + i + 1)
                        d = part[:, 2 * i:2 * i + 2, :].rearrange("p t c -> p (t c)")
                        dve.tensor_tensor(d, psD[i][:, :], d, ALU.add).then_inc(down_drained, 1)
                    assert steps[0] == CHAIN - 2, steps

            over_batches(dve, body)
            dve.wait_ge(keep["step"], B)
            dve.wait_ge(slot_ready, B)
            dve.tensor_copy(keep["counts"][:, :], running[:, :]).then_inc(vec_setup, 1)
            dve.tensor_copy(keep["starts"][:, :], run0[:, :]).then_inc(vec_setup, 1)
            dve.wait_ge(vec_setup, 5 + KC + 2)

        @block.tensor
        def _(pe):
            pe.wait_ge(loaded, 16 * NL)
            pe.wait_ge(pool_setup, 10)
            for k in range(KC):
                for a in range(TAPS):
                    last = pe.transpose(psT[k][:, a * I:(a + 1) * I], conv_raw[:, k * P:(k + 1) * P, a], ident[:, :])
            last.then_inc(pe_setup, 1)
            pe.wait_ge(vec_setup, 5 + KC)

            def body(kind, b, par):
                cur, nxt = flags(kind)
                n = after(kind, b)
                if cur:
                    if kind != "first":
                        pe.wait_ge(h_ready, b)
                    for a in range(TAPS):
                        for k in range(KC):
                            pe.matmul(psG[:, :], conv[:, k, a, :], xT[:, k, a:a + T], start=(a == 0 and k == 0),
                                      stop=(a == TAPS - 1 and k == KC - 1))
                    for k in range(KC):
                        last = pe.matmul(psU[:, :], up[:, k, :], xT[:, k, PAD:], start=(k == 0), stop=(k == KC - 1))
                    last.then_inc(gu_filled, 1)
                if nxt:
                    q = 1 - par if cur else 0
                    pe.wait_ge(xn_ready, n + 1)
                    for k in range(KC):
                        for t in range(QT):
                            last = pe.transpose(psT[k][:, t * P:(t + 1) * P], xn[q][:, t, k * P:(k + 1) * P], ident[:, :])
                        last.then_inc(xT_filled, 1)
                    pe.wait_ge(xT_drained, 2 * (n + 1))
                    if cur:
                        pe.wait_ge(step, b * CHAIN1 + 1)
                    for t in range(QT):
                        for k in range(KC):
                            last = pe.matmul(psR[:, t * E:(t + 1) * E], xT[:, k, PAD + t * P:PAD + (t + 1) * P], wr[:, k, :],
                                             start=(k == 0), stop=(k == KC - 1))
                    last.then_inc(router_filled, 1)
                if cur:
                    pe.wait_ge(hot_ready, b + 1)
                    for t in range(QT + 1):
                        srcs = [(before, t)] if t < QT else []
                        srcs += [(ones, u) for u in range(t)]
                        for i, (m, u) in enumerate(srcs):
                            last = pe.matmul(psRank[:, t * E:(t + 1) * E], m[:, :], both[:, u, :], start=(i == 0),
                                             stop=(i == len(srcs) - 1))
                    last.then_inc(rank_filled, 1)
                    pe.wait_ge(h_ready, b + 1)
                    if kind != "first":
                        pe.wait_ge(down_drained, 2 * b)
                    for i in range(2):
                        for t in range(2):
                            last = pe.matmul(psD[i][:, t * C:(t + 1) * C], h[:, (2 * i + t) * P:(2 * i + t + 1) * P],
                                             down[:, :], start=True, stop=True)
                        last.then_inc(down_filled, 1)

            CHAIN1 = 17
            over_batches(pe, body)


LANES = 4


def expert_tiles(N, ER):
    return (2 * N // P + ER + LANES) // LANES * LANES


def expert_phase(nc, W, sc, keep, N):
    ER, C, I = W["expert_gate_w"].shape
    E = ER + 1
    KC = C // P
    NT = expert_tiles(N, ER)
    xn_rows, lists, results = sc["xn_rows"], sc["lists"], sc["results"]

    with ExitStack() as st:
        def sb(name, shape, dt=F32):
            return st.enter_context(nc.sbuf_tensor(name, shape, dt))

        def ps(name):
            return st.enter_context(nc.psum_tensor(name, [P, 512], F32))

        def sem(name):
            return st.enter_context(nc.semaphore(name))

        passed = sem("passed_expert")
        wgu = sb("wgu", [P, ER, KC, 2, I])
        wd = sb("wd", [P, ER, C])
        ident = sb("ident3", [P, P])
        tiles = sb("tiles", [P, E])
        tiles_i = sb("tiles_i", [P, E], I32)
        ends = [sb(f"ends{i}", [P, E]) for i in range(2)]
        num_i, num = sb("num_i", [1, NT], I32), sb("num", [1, NT])
        ge = sb("ge", [1, NT, ER])
        jump = sb("jump", [P, E])
        spare_row = sb("spare_row", [P, 1])
        row = keep["row"][:, :, :].rearrange("p b t -> p (b t)")
        ROWS = row.shape[1]
        past = sb("past", [P, ROWS, ER])
        back = sb("back", [P, ROWS])
        jumps = sb("jumps", [1, NT, ER])
        expert, offset = sb("expert", [1, NT]), sb("offset", [1, NT])
        NSTEP = NT + 4
        table = sb("table", [1, NSTEP, 4], I32)
        rows_i = sb("rows_i", [1, NT], I32)
        idx = [sb(f"idx{r}", [P, 1], I32) for r in range(LANES)]
        xg = [sb(f"xg{r}", [P, C]) for r in range(LANES)]
        xT = [sb(f"xTe{r}", [P, KC, P]) for r in range(2)]
        sg = [sb(f"sg{r}", [P, I]) for r in range(2)]
        hh = [sb(f"hh{r}", [P, I]) for r in range(2)]
        hT = [sb(f"hT{r}", [P, P]) for r in range(2)]
        yo = [sb(f"yo{r}", [P, C]) for r in range(LANES)]
        psX = [ps(f"psX{r}") for r in range(2)]
        psGU = [ps(f"psGU{r}") for r in range(2)]
        psH = [ps(f"psH{r}") for r in range(2)]
        psY = [ps(f"psY{r}") for r in range(2)]

        weights_in, pool_setup, table_step, table_ready = sem("c_weights"), sem("c_pool"), sem("table_step"), sem("table_ready")
        rows_ready = sem("rows_ready")
        idx_in = [sem(f"idx_in{r}") for r in range(LANES)]
        x_in = [sem(f"xg_in{r}") for r in range(LANES)]
        xT_filled, xT_drained = sem("cxT_filled"), sem("cxT_drained")
        gu_filled, silu_ready, h_ready = sem("cgu_filled"), sem("silu_ready"), sem("ch_ready")
        hT_filled, hT_drained = sem("hT_filled"), sem("hT_drained")
        y_filled, y_drained = sem("cy_filled"), sem("cy_drained")
        y_saved = [sem(f"cy_saved{r}") for r in range(LANES)]

        block = st.enter_context(nc.Block())

        @block.sync
        def _(sp):
            for k in range(KC):
                for m, n in enumerate(("expert_gate_w", "expert_up_w")):
                    sp.dma_start(wgu[:, :, k, m, :], W[n][:, k * P:(k + 1) * P, :].rearrange("e p i -> p e i")).then_inc(weights_in, 16)
            sp.dma_start(wd[:, :, :], W["expert_down_w"].rearrange("e i c -> i e c")).then_inc(weights_in, 16)
            sp.wait_ge(rows_ready, 1)
            sp.wait_ge(table_ready, 1)
            LAG = 2 * LANES

            def fetch(i, r, k):
                if not isinstance(k, int) or k > 0:
                    sp.wait_ge(x_in[r], 16 * k)
                row = sp.value_load(rows_i[0:1, bass.ds(i, 1)], min_val=0, max_val=ER * N)
                sp.dma_start(idx[r][:, :], lists[bass.ds(row, P), :]).then_inc(idx_in[r], 16)

            def save(i, r):
                sp.wait_ge(y_drained, i + 1)
                sp.dma_start(results.rearrange("(n p) c -> n p c", p=P)[i], yo[r][:, :]).then_inc(y_saved[r], 16)

            for k in range(2):
                for r in range(LANES):
                    fetch(k * LANES + r, r, k)
            with sp.Fori(2, NT // LANES) as k:
                for r in range(LANES):
                    save((k - 2) * LANES + r, r)
                    fetch(k * LANES + r, r, k)
            for i in range(NT - LAG, NT):
                save(i, i % LANES)
            for r in range(LANES):
                sp.wait_ge(y_saved[r], 16 * NT // LANES)

        @block.gpsimd
        def _(pool):
            pool.memset(ident[:, :], 0.0).then_inc(pool_setup, 1)
            pool.memset(table[:, :, :], 0).then_inc(pool_setup, 1)
            pool.iota(num_i[:, :], pattern=[[1, NT]], base=0, channel_multiplier=0).then_inc(pool_setup, 1)
            pool.iota(jump[:, :], pattern=[[0, E]], base=N, channel_multiplier=0,
                      allow_small_or_imprecise_dtypes=True).then_inc(pool_setup, 1)
            pool.wait_ge(pool_setup, 4)
            pool.affine_select(out=ident[:, :], in_=ident[:, :], compare_op=ALU.not_equal, fill=1.0, base=0,
                               pattern=[[-1, P]], channel_multiplier=1).then_inc(pool_setup, 1)

            def gather(r, k):
                if not isinstance(k, int) or k > 0:
                    pool.wait_ge(xT_filled, (k - 1) * LANES + r + 1)
                pool.wait_ge(idx_in[r], 16 * (k + 1))
                pool.sem_inc(passed, 1)
                pool.indirect_dma_start(out=xg[r][:, :], out_offset=None, in_=xn_rows[:, :],
                                        in_offset=bass.IndirectOffsetOnAxis(ap=idx[r][:, 0:1], axis=0)).then_inc(x_in[r], 16)

            for r in range(LANES):
                gather(r, 0)
            with pool.Fori(1, NT // LANES) as k:
                for r in range(LANES):
                    gather(r, k)

        def over_tiles(eng, step):
            for j in range(LANES):
                step(j, j, [j >= s for s in range(4)])
            with eng.Fori(1, NT // LANES) as k:
                for r in range(LANES):
                    step(k * LANES + r, r, [True] * 4)
            for j in range(NT, NT + 3):
                step(j, j % LANES, [j - s < NT for s in range(4)])

        @block.scalar
        def _(act):
            def step(j, r, on):
                if on[0]:
                    act.wait_ge(xT_filled, j + 1)
                    if not isinstance(j, int) or j >= 2:
                        act.wait_ge(gu_filled, j - 1)
                    act.activation(xT[r % 2][:, :, :].rearrange("p k t -> p (k t)"), psX[r % 2][:, 0:C],
                                   ACT.Copy).then_inc(xT_drained, 1)
                if on[1]:
                    q = (r - 1) % 2
                    act.wait_ge(gu_filled, j)
                    if not isinstance(j, int) or j >= 3:
                        act.wait_ge(h_ready, j - 2)
                    act.activation(sg[q][:, :], psGU[q][:, 0:I], ACT.Silu).then_inc(silu_ready, 1)
                if on[3]:
                    q = (r - 3) % 2
                    act.wait_ge(y_filled, j - 2)
                    lane = (r - 3) % LANES
                    if not isinstance(j, int) or j - 3 >= LANES:
                        act.wait_ge(y_saved[lane], rounds(j, r) * 16)
                    act.activation(yo[lane][:, :], psY[q][:, 0:C], ACT.Copy).then_inc(y_drained, 1)

            def rounds(j, r):
                if isinstance(j, int):
                    return (j - 3) // LANES
                return round_of[0] if r == 3 else round_of[0] - 1

            round_of = [None]
            for j in range(LANES):
                step(j, j, [j >= s for s in range(4)])
            for r in range(LANES):
                step(LANES + r, r, [True] * 4)
            with act.Fori(2, NT // LANES) as k:
                round_of[0] = k
                for r in range(LANES):
                    step(k * LANES + r, r, [True] * 4)
            for j in range(NT, NT + 3):
                step(j, j % LANES, [j - s < NT for s in range(4)])

        @block.vector
        def _(dve):
            n = [0]

            def link(ins):
                n[0] += 1
                ins.then_inc(table_step, 1)
                dve.wait_ge(table_step, n[0])

            dve.wait_ge(pool_setup, 4)
            counts, starts = keep["counts"][:, :], keep["starts"][:, :]
            link(dve.tensor_copy(num[:, :], num_i[:, :]))
            link(dve.tensor_tensor(tiles[:, :], counts, starts, ALU.subtract))
            link(dve.tensor_scalar(tiles[:, :], tiles[:, :], float(P - 1), None, ALU.add))
            link(dve.tensor_copy(tiles_i[:, :], tiles[:, :]))
            link(dve.tensor_scalar(tiles_i[:, :], tiles_i[:, :], 7, None, ALU.logical_shift_right))
            link(dve.tensor_copy(tiles[:, :], tiles_i[:, :]))
            link(dve.tensor_copy(ends[0][:, :], tiles[:, :]))
            src = 0
            for d in (1, 2, 4, 8):
                link(dve.tensor_copy(ends[1 - src][:, 0:d], ends[src][:, 0:d]))
                link(dve.tensor_tensor(ends[1 - src][:, d:E], ends[src][:, d:E], ends[src][:, 0:E - d], ALU.add))
                src = 1 - src
            link(dve.scalar_tensor_tensor(out=jump[:, :], in0=tiles[:, :], scalar=-float(P), in1=jump[:, :],
                                          op0=ALU.mult, op1=ALU.add))
            bc = [1, NT, ER]
            link(dve.tensor_tensor(ge[:, :, :], num[:, :].unsqueeze(2).to_broadcast(bc),
                                   ends[src][0:1, 0:ER].unsqueeze(1).to_broadcast(bc), ALU.is_ge))
            link(dve.tensor_tensor(jumps[:, :, :], ge[:, :, :], jump[0:1, 0:ER].unsqueeze(1).to_broadcast(bc), ALU.mult))
            link(dve.tensor_reduce(expert[:, :], ge[:, :, :], axis=AX, op=ALU.add))
            link(dve.tensor_reduce(offset[:, :], jumps[:, :, :], axis=AX, op=ALU.add))
            link(dve.scalar_tensor_tensor(out=offset[:, :], in0=num[:, :], scalar=float(P), in1=offset[:, :],
                                          op0=ALU.mult, op1=ALU.add))
            link(dve.tensor_scalar(offset[:, :], offset[:, :], float(ER * N), None, ALU.min))
            link(dve.tensor_scalar(expert[:, :], expert[:, :], float(ER - 1), None, ALU.min))
            dve.tensor_copy(rows_i[:, :], offset[:, :]).then_inc(rows_ready, 1)
            link(dve.tensor_scalar(table[:, 1:NT + 1, 0], expert[:, :], float(KC * 2 * I), None, ALU.mult))
            dve.tensor_scalar(table[:, 3:NT + 3, 1], expert[:, :], float(C), None, ALU.mult).then_inc(table_ready, 1)
            bc = [P, ROWS, ER]
            link(dve.tensor_tensor(past[:, :, :], row.unsqueeze(2).to_broadcast(bc),
                                   starts[:, 1:E].unsqueeze(1).to_broadcast(bc), ALU.is_ge))
            link(dve.tensor_tensor(past[:, :, :], past[:, :, :], jump[:, 0:ER].unsqueeze(1).to_broadcast(bc), ALU.mult))
            link(dve.tensor_reduce(back[:, :], past[:, :, :], axis=AX, op=ALU.add))
            link(dve.tensor_scalar(spare_row[:, :], ends[src][:, ER - 1:ER], float(P), None, ALU.mult))
            link(dve.tensor_tensor(back[:, :], row, back[:, :], ALU.subtract))
            link(dve.tensor_scalar(row, back[:, :], spare_row[:, 0:1], None, ALU.min))

            def step(j, r, on):
                if on[1]:
                    q = (r - 1) % 2
                    dve.wait_ge(silu_ready, j)
                    if not isinstance(j, int) or j >= 3:
                        dve.wait_ge(hT_filled, j - 2)
                    dve.tensor_tensor(hh[q][:, :], sg[q][:, :], psGU[q][:, I:2 * I], ALU.mult).then_inc(h_ready, 1)
                if on[2]:
                    q = (r - 2) % 2
                    dve.wait_ge(hT_filled, j - 1)
                    if not isinstance(j, int) or j >= 4:
                        dve.wait_ge(y_filled, j - 3)
                    dve.tensor_copy(hT[q][:, :], psH[q][:, 0:P]).then_inc(hT_drained, 1)

            over_tiles(dve, step)

        @block.tensor
        def _(pe):
            pe.wait_ge(weights_in, 16 * 5)
            pe.wait_ge(pool_setup, 5)
            pe.wait_ge(table_ready, 1)
            wgu_flat = wgu[:, :, :, :, :].rearrange("p e k m i -> p (e k m i)")
            wd_flat = wd[:, :, :].rearrange("p e c -> p (e c)")

            def step(j, r, on):
                if on[1] or on[3]:
                    at = pe.value_load(table[0:1, bass.ds(j, 1), 0], min_val=0, max_val=(ER - 1) * KC * 2 * I)
                    down_at = pe.value_load(table[0:1, bass.ds(j, 1), 1], min_val=0, max_val=(ER - 1) * C)
                if on[0]:
                    if not isinstance(j, int) or j >= 2:
                        pe.wait_ge(xT_drained, j - 1)
                    k = j if isinstance(j, int) else None
                    pe.wait_ge(x_in[r], 16 * (j // LANES + 1) if k is not None else 16 * (round_of[0] + 1))
                    for c in range(KC):
                        last = pe.transpose(psX[r % 2][:, c * P:(c + 1) * P], xg[r][:, c * P:(c + 1) * P], ident[:, :])
                    last.then_inc(xT_filled, 1)
                if on[1]:
                    q = (r - 1) % 2
                    pe.wait_ge(xT_drained, j)
                    if not isinstance(j, int) or j >= 3:
                        pe.wait_ge(h_ready, j - 2)
                    for c in range(KC):
                        last = pe.matmul(psGU[q][:, 0:2 * I], xT[q][:, c, :], wgu_flat[:, bass.ds(at + c * 2 * I, 2 * I)],
                                         start=(c == 0), stop=(c == KC - 1))
                    last.then_inc(gu_filled, 1)
                if on[2]:
                    q = (r - 2) % 2
                    pe.wait_ge(h_ready, j - 1)
                    if not isinstance(j, int) or j >= 4:
                        pe.wait_ge(hT_drained, j - 3)
                    pe.transpose(psH[q][:, 0:P], hh[q][:, :], ident[:, :]).then_inc(hT_filled, 1)
                if on[3]:
                    q = (r - 3) % 2
                    pe.wait_ge(hT_drained, j - 2)
                    if not isinstance(j, int) or j >= 5:
                        pe.wait_ge(y_drained, j - 4)
                    pe.matmul(psY[q][:, 0:C], hT[q][:, :], wd_flat[:, bass.ds(down_at, C)], start=True,
                              stop=True).then_inc(y_filled, 1)

            round_of = [None]
            for j in range(LANES):
                step(j, j, [j >= s for s in range(4)])
            for r in range(LANES):
                step(LANES + r, r, [True] * 4)
            with pe.Fori(2, NT // LANES) as k:
                round_of[0] = k
                for r in range(LANES):
                    step(k * LANES + r, r, [True] * 4)
            for j in range(NT, NT + 3):
                step(j, j % LANES, [j - s < NT for s in range(4)])


def combine_phase(nc, sc, keep, out):
    B, T, C = out.shape
    QT = T // P
    acc, results = sc["acc"], sc["results"]
    with ExitStack() as st:
        def sb(name, shape, dt=F32):
            return st.enter_context(nc.sbuf_tensor(name, shape, dt))

        def sem(name):
            return st.enter_context(nc.semaphore(name))

        passed = sem("passed_combine")
        at = [sb(f"at{i}", [P, QT, C]) for i in range(2)]
        got = [sb(f"got{i}", [P, 2, QT, C]) for i in range(2)]
        rows = [sb(f"rows{i}", [P, 2 * QT], U32) for i in range(2)]
        w = [sb(f"wt{i}", [P, QT, 2]) for i in range(2)]
        acc_in = [sem(f"d_acc_in{i}") for i in range(2)]
        rows_ready, first_done, done = sem("d_rows_ready"), sem("d_first_done"), sem("d_done")
        got_in = [sem(f"got_in{i}") for i in range(2)]
        saved = [sem(f"d_saved{i}") for i in range(2)]
        block = st.enter_context(nc.Block())

        @block.sync
        def _(sp):
            def load(b, i):
                sp.dma_start(at[i][:, :, :], acc[b].rearrange("(t p) c -> p t c", p=P)).then_inc(acc_in[i], 16)

            def save(b, i):
                sp.wait_ge(done, b + 1)
                sp.dma_start(out[b].rearrange("(t p) c -> p t c", p=P), at[i][:, :, :]).then_inc(saved[i], 16)

            for i in range(2):
                load(i, i)
            with sp.Fori(1, B // 2) as k:
                for i in range(2):
                    save(2 * k - 2 + i, i)
                for i in range(2):
                    sp.wait_ge(saved[i], 16 * k)
                    load(2 * k + i, i)
            for i in range(2):
                save(B - 2 + i, i)
                sp.wait_ge(saved[i], 16 * B // 2)

        @block.gpsimd
        def _(pool):
            with pool.Fori(0, B // 2) as k:
                for i in range(2):
                    pool.wait_ge(rows_ready, 2 * k + i + 1)
                    pool.sem_inc(passed, 1)
                    for m in range(2):
                        for t in range(QT):
                            c = m * QT + t
                            pool.indirect_dma_start(
                                out=got[i][:, m, t, :], out_offset=None, in_=results[:, :],
                                in_offset=bass.IndirectOffsetOnAxis(ap=rows[i][:, c:c + 1], axis=0)).then_inc(got_in[i], 16)

        @block.vector
        def _(dve):
            def rows_of(b, i):
                dve.tensor_copy(w[i][:, :, :], keep["weight"][:, bass.ds(b * QT, QT), :])
                dve.tensor_copy(rows[i][:, :].rearrange("p (m t) -> p m t", m=2),
                                keep["row"][:, bass.ds(b * 2, 2), :]).then_inc(rows_ready, 1)

            def sums(b, i, k):
                dve.wait_ge(rows_ready, b + 1)
                dve.wait_ge(acc_in[i], 16 * (k + 1))
                dve.wait_ge(got_in[i], 16 * 2 * QT * (k + 1))
                for m in range(2):
                    if m == 1:
                        dve.wait_ge(first_done, b + 1)
                    for t in range(QT):
                        last = dve.scalar_tensor_tensor(out=at[i][:, t, :], in0=got[i][:, m, t, :], scalar=w[i][:, t, m:m + 1],
                                                        in1=at[i][:, t, :], op0=ALU.mult, op1=ALU.add)
                    last.then_inc(first_done if m == 0 else done, 1)
                dve.wait_ge(done, b + 1)

            for i in range(2):
                rows_of(i, i)
            with dve.Fori(0, B // 2 - 1) as k:
                for i in range(2):
                    sums(2 * k + i, i, k)
                    rows_of(2 * k + 2 + i, i)
            for i in range(2):
                sums(B - 2 + i, i, B // 2 - 1)


def flamingo_gated_block(nc, x, ctx_512, g_xattn, g_ffn, Wk, bk, Wq, bq, Wv, bv, Wck, bck, Wcq, bcq, Wcv, bcv, Wp, bp,
                         router_w, router_bias, expert_gate_w, expert_up_w, expert_down_w, conv_w, shared_up_w,
                         shared_down_w, out):
    B, T, C = x.shape
    N, QT, E = B * T, T // P, router_w.shape[1]
    attention = dict(Wk=Wk, bk=bk, Wq=Wq, bq=bq, Wv=Wv, bv=bv, Wck=Wck, bck=bck, Wcq=Wcq, bcq=bcq, Wcv=Wcv, bcv=bcv,
                     Wp=Wp, bp=bp)
    ffn = dict(router_w=router_w, router_bias=router_bias, expert_gate_w=expert_gate_w, expert_up_w=expert_up_w,
               expert_down_w=expert_down_w, conv_w=conv_w, shared_up_w=shared_up_w, shared_down_w=shared_down_w)

    def dram(name, shape, dt=F32):
        return nc.dram_tensor(name, shape, dt, kind="Internal").ap()

    x1 = dram("x1", (B, T, C))
    scratch = dict(
        xn_rows=dram("xn_rows", (N, C)), acc=dram("acc", (B, T, C)),
        lists=dram("lists", (E * N + P, 1), I32),
        results=dram("results", (expert_tiles(N, E - 1) * P, C)))

    attention_phase(nc, x, ctx_512, g_xattn, attention, x1)
    with ExitStack() as st:
        keep = dict(weight=st.enter_context(nc.sbuf_tensor("keep_weight", [P, B * QT, 2], F32)),
                    row=st.enter_context(nc.sbuf_tensor("keep_row", [P, B * 2, QT], F32)),
                    counts=st.enter_context(nc.sbuf_tensor("keep_counts", [P, E], F32)),
                    starts=st.enter_context(nc.sbuf_tensor("keep_starts", [P, E], F32)),
                    step=st.enter_context(nc.semaphore("slots_summed")))
        routing_phase(nc, x1, g_ffn, ffn, scratch, keep)
        expert_phase(nc, ffn, scratch, keep, N)
        combine_phase(nc, scratch, keep, out)


_INS = ['x', 'ctx_512', 'g_xattn', 'g_ffn', 'L0_xattn_Wk', 'L0_xattn_bk', 'L0_xattn_Wq', 'L0_xattn_bq', 'L0_xattn_Wv',
        'L0_xattn_bv', 'L0_xattn_Wck', 'L0_xattn_bck', 'L0_xattn_Wcq', 'L0_xattn_bcq', 'L0_xattn_Wcv', 'L0_xattn_bcv',
        'L0_xattn_Wp', 'L0_xattn_bp', 'L0_ffn_router_w', 'L0_ffn_router_bias', 'L0_ffn_expert_gate_w',
        'L0_ffn_expert_up_w', 'L0_ffn_expert_down_w', 'L0_ffn_conv_w', 'L0_ffn_shared_up_w', 'L0_ffn_shared_down_w']
_OUTS = [((16, 512, 256), 'float32')]


def kernel(**inputs):
    import numpy as _np
    import concourse.bacc as _bacc
    from concourse import mybir as _mybir
    from concourse.bass_utils import run_bass_kernel_spmd as _run

    nc = _bacc.Bacc("TRN2", target_bir_lowering=False, num_devices=1)
    arrays, args = {}, []
    for name in _INS:
        a = _np.ascontiguousarray(inputs[name])
        arrays[f"in_{name}_dram"] = a
        args.append(nc.dram_tensor(f"in_{name}_dram", a.shape, _mybir.dt.from_np(a.dtype), kind="ExternalInput").ap())
    for i, (shape, dtype) in enumerate(_OUTS):
        dt = _mybir.dt.from_np(_np.dtype(dtype))
        args.append(nc.dram_tensor(f"out_{i}_dram", shape, dt, kind="ExternalOutput").ap())
    flamingo_gated_block(nc, *args)
    r = _run(nc, [arrays], core_ids=[0])
    return r.results[0]["out_0_dram"]
```

```python
from contextlib import ExitStack

import concourse.bass as bass
from concourse import mybir

ALU = mybir.AluOpType
ACT = mybir.ActivationFunctionType
F32 = mybir.dt.float32
BF16 = mybir.dt.bfloat16
I32 = mybir.dt.int32
U32 = mybir.dt.uint32
AX = mybir.AxisListType.X

P = 128
HEAD_GROUP = 4
BIG = 1.0e30
EPS = 1e-5


PARTS = {
    "pro": (False, False, True), "first": (False, True, True), "mid": (True, True, True),
    "last": (True, True, False), "post": (True, False, False),
}


class Events:

    def __init__(self, names, last_batch, credit=0):
        self.names = names
        self.last_batch = last_batch
        self.credit = credit

    def start(self, kind, b):
        n = {k: len(self.names(k)) for k in PARTS}
        if kind == "pro":
            return self.credit
        if kind == "first":
            return self.credit + n["pro"]
        if kind == "mid":
            return self.credit + n["pro"] + n["first"] + (b - 1) * n["mid"]
        end = self.credit + n["pro"] + n["first"] + (self.last_batch - 1) * n["mid"]
        return end if kind == "last" else end + n["last"]

    def upto(self, kind, b, name):
        return self.start(kind, b) + self.names(kind).index(name) + 1

    def slot(self, kind, name, ring):
        before = self.start(kind, 1) - self.credit
        return (before + self.names(kind).index(name)) % ring


ROUTE_UNITS = {(0, 13): ("rT", 0), (0, 14): ("rT", 1), (0, 15): ("rT", 2), (0, 16): ("rT", 3), (0, 18): ("rl",), (1, 10): ("rk",)}
ROUTE_STEPS = {(0, 0): "stats", (0, 2): "aggregate", (0, 10): "normalise", (0, 19): "max", (0, 20): "shift", (0, 23): "sum",
               (1, 0): "invert", (1, 1): "probs", (1, 2): "top", (1, 3): "index", (1, 4): "as float",
               (1, 5): "hot", (1, 6): "both", (1, 7): "weigh", (1, 8): "identity", (1, 11): "weights", (1, 12): "at",
               (1, 13): "slots", (1, 14): "keep"}
ROUTE_EXP = 21
LN_SUMS, LN_ROWS = (1, 15), (1, 22)


def attention_phase(nc, x, ctx, g_xattn, W, x1s, g_ffn, router_w, router_bias, xn_rows, lists, keep):
    B, T, C = x.shape
    TC, CC = ctx.shape[1:]
    H, D = 16, C // 16
    E, N = router_w.shape[1], B * T
    KC, QT = C // P, T // P
    HU = H // KC
    ALLC = 3 * T + TC
    Q0, CQ0, K0, KC0 = 0, T, 2 * T, 3 * T
    COLS = (slice(Q0, CQ0), slice(CQ0, K0), slice(K0, KC0), slice(KC0, ALLC))
    STACK, MROWS = 6 * D, 3
    SCALE = 1.0 / D ** 0.5
    RING = 3
    assert KC == 2 and QT == 4 and HU * D == P and 2 * TC == P and CC == P

    GROUP = [("X", 0), ("X", 1), ("A", 0), ("B", 0), ("A", 1), ("B", 1), ("C", 0),
             ("A", 2), ("B", 2), ("A", 3), ("B", 3), ("C", 2)]
    PT_SLOT = {n: i for i, n in enumerate(GROUP[2:])}
    NST = 2 * len(GROUP)
    MAXU = []
    for qt in range(QT):
        MAXU.append(("cross", qt, 0, HU))
        n = {0: 4, 1: 2, 2: 1, 3: 1}[qt]
        MAXU += [("self", qt, h, n) for h in range(0, HU, n)]
    NSM = len(MAXU)
    SM_PRE, SM_MID = 6, NSM
    BESIDE = [[u for u in range(SM_PRE, SM_MID) if (u - SM_PRE) * NST // (SM_MID - SM_PRE) == k] for k in range(NST)]

    def scalar_units(kind):
        prev, cur, nxt = PARTS[kind]
        out = []
        for c in range(KC):
            if nxt and c == 0:
                out += [("xT", t) for t in range(QT)]
            if nxt:
                out += [("proj", c, i) for i in range(4)]
            if cur:
                out += [("st", c, k) for k in range(NST)]
        return out

    def slots(c, name, work, prev):
        out = []
        for k in range(NST):
            if work:
                out += [name + (u,) for u in BESIDE[k]]
            if prev and (c, k) in ROUTE_UNITS:
                out.append(ROUTE_UNITS[c, k])
        return out

    def vector_units(kind):
        prev, cur, nxt = PARTS[kind]
        out = []
        if cur:
            out += [("v", 1), ("vc", 1)]
        if prev:
            out += [("tU", 1, 1, "x"), ("tU", 1, 1, "s")]
        if cur:
            out += [("mT", 0)] + [("sm", 1, k) for k in range(2)]
        if prev:
            out += [("yT", k) for k in range(KC)]
        if cur:
            out += [("sm", 1, k) for k in range(2, SM_PRE)]
        if prev:
            out += [("wp", t) for t in range(QT)]
        out += slots(0, ("sm", 1), cur, prev)
        if cur:
            out += [("tU", 0, 0, "x"), ("tU", 0, 0, "s")]
            out += [("sm", 1, k) for k in range(SM_MID, NSM)]
        if nxt:
            out += [("v", 0), ("vc", 0)]
        if cur:
            out += [("tU", 0, 1, "x"), ("tU", 0, 1, "s"), ("mT", 1)]
        if nxt:
            out += [("sm", 0, k) for k in range(SM_PRE)]
        out += slots(1, ("sm", 0), nxt, prev)
        if cur:
            out += [("tU", 1, 0, "x"), ("tU", 1, 0, "s")]
        if nxt:
            out += [("sm", 0, k) for k in range(SM_MID, NSM)]
        return out

    def of_current(names):
        return lambda kind: names if PARTS[kind][1] else []

    def of_next(names):
        return lambda kind: names if PARTS[kind][2] else []

    LB = B - 1
    SU, VU = Events(scalar_units, LB), Events(vector_units, LB)
    assert len(scalar_units("mid")) % RING == 0 and len(vector_units("mid")) % RING == 0
    PV = Events(of_current([(w, c, g) for c in range(KC) for g in range(2) for w in ("x", "s")]), LB, credit=8)
    MASKED = Events(of_current([(c, g, s) for c in range(KC) for g in range(2) for s in range(10)]), LB)
    YADD = Events(lambda kind: ([(1, 1)] if PARTS[kind][0] else []) + ([(0, 0), (0, 1), (1, 0)] if PARTS[kind][1] else []),
                  LB, credit=4)
    SPLIT = Events(of_next([0, 1]), LB)
    MSPLIT = Events(of_current([0, 1]), LB)
    LN = Events(of_next([0]), LB)

    scr = nc.dram_tensor("qk_scratch", (KC, 3, P, ALLC), BF16, kind="Internal").ap()
    mscr = nc.dram_tensor("max_scratch", (KC, 3, HU * 2 * T), BF16, kind="Internal").ap()

    with ExitStack() as st:
        def sb(name, shape, dt=F32):
            return st.enter_context(nc.sbuf_tensor(name, shape, dt))

        def sem(name):
            return st.enter_context(nc.semaphore(name))

        banks_s = [st.enter_context(nc.psum_tensor(f"scalar_bank{i}", [P, 512], F32)) for i in range(RING)]
        banks_v = [st.enter_context(nc.psum_tensor(f"vector_bank{i}", [P, 512], F32)) for i in range(RING)]
        pv_self = st.enter_context(nc.psum_tensor("pv_self", [P, 512], F32))
        pv_cross = st.enter_context(nc.psum_tensor("pv_cross", [P, 512], F32))

        wq = {n: sb(f"w_{n}", [P, KC, KC, P]) for n in ("q", "cq", "k")}
        wck = sb("w_ck", [P, KC, P])
        wv = sb("w_v", [P, KC, C])
        wcv = sb("w_cv", [P, C])
        wp = sb("w_p", [P, KC, C])
        bias_rows = sb("bias_rows", [8, P])
        bias_perm = sb("bias_perm", [8, P])
        bias = sb("bias", [P, 8])
        bv = sb("bv", [P, KC, QT, P])
        bcv = sb("bcv", [P, C])
        bpg = sb("bpg", [P, C])
        gate = sb("gate", [P, 1])
        ident = sb("ident", [P, P])
        ident_b = sb("ident_b", [P, P], BF16)
        tri = sb("tri", [P, 4, P], BF16)
        half = sb("half", [P, QT])

        xt = sb("xt", [P, QT, C])
        stats = sb("stats", [P, QT, 6])
        mv = sb("mv", [P, QT, 2])
        rstd = sb("rstd", [P, QT])
        xn = sb("xn", [P, QT, C])
        xnT = sb("xnT", [P, KC, T])
        ctile = sb("ctile", [P, CC])
        ctxT = sb("ctxT", [P, P])
        q32 = sb("q32", [P, ALLC])
        parts = sb("parts", [P, 3, ALLC], BF16)
        stack = [sb(f"stack{c}", [P, HU, ALLC], BF16) for c in range(KC)]
        vst = sb("vst", [P, QT, KC, HU, 32])
        vcst = sb("vcst", [P, KC, HU // 2, 64])
        nmax = [sb(f"nmax{c}", [P, QT, HU, 2]) for c in range(KC)]
        mres = sb("mres", [P, QT, HU * 2])
        mparts = sb("mparts", [P, QT, 3, HU * 2], BF16)
        mT = [sb(f"mT{c}", [3 * HU * 2, T], BF16) for c in range(KC)]
        pt = [sb(f"pt{g}", [P, 10, 512]) for g in range(2)]
        ct = [sb(f"ct{g}", [P, 2, 512]) for g in range(2)]
        usum = {(w, g): sb(f"usum_{w}{g}", [P, T]) for w in ("x", "s") for g in range(2)}
        recip = {w: sb(f"recip_{w}", [P, QT, HEAD_GROUP]) for w in ("x", "s")}
        y = sb("y", [P, QT, H, D])
        yc = [sb(f"yc{g}", [P, QT, HEAD_GROUP, D]) for g in range(2)]
        yT = sb("yT", [P, KC, T])
        xr = sb("xr", [P, QT, C])
        xn2 = sb("xn2", [P, QT, C])
        xT2 = sb("xT2", [P, KC, T])
        stats2, mv2, rstd2 = sb("stats2", [P, QT, 6]), sb("mv2", [P, QT, 2]), sb("rstd2", [P, QT])
        wr, rb, gate2 = sb("router_w", [P, KC, E]), sb("router_b", [P, QT, E]), sb("gate2", [P, 1])
        before, ones = sb("before", [P, P], BF16), sb("ones", [P, P], BF16)
        NFILL = lists.shape[0] // P
        zeros = sb("zeros", [P, NFILL], I32)
        iota_i, iota = sb("iota_i", [P, QT, E], I32), sb("iota", [P, QT, E])
        tok_i, tok = sb("tok_i", [P, QT], I32), sb("tok", [P, QT])
        logit, prob = sb("logit", [P, QT, E]), sb("prob", [P, QT, E])
        m4, z4, s4 = sb("m4", [P, QT]), sb("z4", [P, QT]), sb("s4", [P, QT])
        top, topi = sb("top", [P, QT, 8]), sb("topi", [P, QT, 8], U32)
        topf, w2, wid2 = sb("topf", [P, QT, 2]), sb("w2", [P, QT, 2]), sb("wid2", [P, QT, 2])
        hot = [sb(f"hot{k}", [P, QT, E]) for k in range(2)]
        both = sb("both", [P, QT, E], BF16)
        place = sb("place", [P, QT, E])
        slotf = sb("slotf", [P, 2, QT])
        slot = sb("slot", [P, 2 * QT], U32)
        slot_i = sb("slot_i", [P, 2 * QT], I32)
        tokens = sb("tokens", [P, QT], I32)
        running = sb("running", [P, E])
        raw = {n: pt[0][:, i, :].rearrange("p (k c) -> p k c", k=KC) for i, n in enumerate(("q", "cq", "k"))}
        raw_ck = pt[0][:, 3, 0:C]

        passed = sem("passed")
        weights_in = sem("weights_in")
        setup_pool = sem("setup_pool")
        setup_vec = sem("setup_vec")
        setup_pe = sem("setup_pe")
        gate_ready = sem("gate_ready")
        scalar_filled = sem("scalar_filled")
        scalar_drained = sem("scalar_drained")
        vector_filled = sem("vector_filled")
        vector_drained = sem("vector_drained")
        pv_filled = sem("pv_filled")
        pv_drained = sem("pv_drained")
        norm_step = sem("norm_step")
        masked = sem("masked")
        y_added = sem("y_added")
        split_done = sem("split_done")
        h_ready = sem("h_ready")
        r_ready = sem("r_ready")
        m_ready = sem("m_ready")
        msplit_done = sem("msplit_done")
        msplit_step = sem("msplit_step")
        x_in = sem("x_in")
        ctx_in = sem("ctx_in")
        xr_in = sem("xr_in")
        xres_ready = sem("xres_ready")
        stats_ready = sem("stats_ready")
        mv_ready = sem("mv_ready")
        rstd_step = sem("rstd_step")
        rstd_ready = sem("rstd_ready")
        xn_ready = sem("xn_ready")
        scr_written = sem("scr_written")
        stack_in = [sem(f"stack_in{c}") for c in range(KC)]
        m_stored = sem("m_stored")
        m_in = [sem(f"m_in{c}") for c in range(KC)]
        x1_stored = sem("x1_stored")

        route_loaded, route_pool, route_vec = sem("route_loaded"), sem("route_pool"), sem("route_vec")
        gate2_ready, lists_zeroed = sem("gate2_ready"), sem("lists_zeroed")
        stats2_ready, mv2_ready, rstd2_step, rstd2_ready = sem("stats2"), sem("mv2"), sem("rstd2_step"), sem("rstd2")
        xn2_ready, xn2_saved = sem("xn2_ready"), sem("xn2_saved")
        logits_shifted, logits_exp, route_step = sem("logits_shifted"), sem("logits_exp"), sem("route_step")
        hot_ready, slot_ready, scattered = sem("hot_ready"), sem("slot_ready"), sem("scattered")
        ROUTE_LOADS = 2 + QT

        NW = 22
        block = st.enter_context(nc.Block())

        def over_batches(eng, body):
            body("pro", 0)
            body("first", 0)
            with eng.Fori(1, B - 1) as b:
                body("mid", b)
            body("last", B - 1)
            body("post", B)

        @block.sync
        def _(sp):
            def load_x(b):
                sp.dma_start(xt[:, :, :], x[b].rearrange("(t p) c -> p t c", p=P)).then_inc(x_in, 16)

            def load_ctx(b):
                for i in range(2):
                    sp.dma_start(ctile[i * TC:(i + 1) * TC, :], ctx[b]).then_inc(ctx_in, 16)

            def load_xr(b):
                sp.dma_start(xr[:, :, :], x[b].rearrange("(t p) c -> p t c", p=P)).then_inc(xr_in, 16)

            def write_parts(kind, b, c):
                sp.wait_ge(split_done, SPLIT.upto(kind, b, c))
                if kind != "pro":
                    sp.wait_ge(stack_in[c], (b + 1) * 7 * 16)
                sp.dma_start(scr[c].rearrange("s p t -> p s t"), parts[:, :, :]).then_inc(scr_written, 16)

            def read_stack(kind, b, c):
                sp.wait_ge(scr_written, 16 * SPLIT.upto(kind, b, c))
                sp.sem_inc(passed, 1)
                if kind != "pro":
                    sp.wait_ge(scalar_filled, SU.upto(kind, b, ("st", c, NST - 1)))
                rows = scr[c].rearrange("s (d h) t -> (s d) h t", h=HU)
                at = 0
                for n in (3, 2, 1):
                    sp.dma_start(stack[c][at:at + n * D, :, 0:K0], rows[0:n * D, :, 0:K0]).then_inc(stack_in[c], 16)
                    at += n * D
                at = 0
                for first, n in ((0, 2), (0, 2), (0, 1), (2, 1)):
                    sp.dma_start(stack[c][at:at + n * D, :, K0:ALLC],
                                 rows[first * D:(first + n) * D, :, K0:ALLC]).then_inc(stack_in[c], 16)
                    at += n * D

            def max_rows(kind, b, c):
                sp.wait_ge(vector_drained, VU.upto(kind, b, ("mT", c)))
                sp.dma_start(mscr[c].rearrange("s (h t) -> (s h) t", t=T), mT[c][:, :]).then_inc(m_stored, 16)
                sp.wait_ge(m_stored, 16 * MSPLIT.upto(kind, b, c))
                sp.dma_start(stack[c][STACK:STACK + MROWS, :, 0:K0],
                             mscr[c].rearrange("s (h t) -> s h t", h=HU)).then_inc(m_in[c], 16)

            load_x(0)
            load_ctx(0)
            wnat = {"q": W["Wq"], "cq": W["Wcq"], "k": W["Wk"]}
            for n, w in wnat.items():
                sp.dma_start(raw[n], w.rearrange("(k p) c -> p k c", p=P)).then_inc(weights_in, 16)
            sp.dma_start(raw_ck, W["Wck"]).then_inc(weights_in, 16)
            sp.dma_start(wv[:, :, :], W["Wv"].rearrange("(k p) c -> p k c", p=P)).then_inc(weights_in, 16)
            sp.dma_start(wcv[:, :], W["Wcv"]).then_inc(weights_in, 16)
            for i, n in enumerate(("bq", "bcq", "bk", "bck")):
                sp.dma_start(bias_rows[2 * i:2 * i + 2, :], W[n].rearrange("(c p) -> c p", p=P)).then_inc(weights_in, 16)
            for c in range(KC):
                for t in range(QT):
                    sp.dma_start(bv[:, c, t, :], W["bv"][c * P:(c + 1) * P].partition_broadcast(P)).then_inc(weights_in, 16)
            sp.dma_start(bcv[:, :], W["bcv"].partition_broadcast(P)).then_inc(weights_in, 16)
            sp.dma_start(bpg[:, :], W["bp"].partition_broadcast(P)).then_inc(weights_in, 16)
            sp.dma_start(gate[:, :], g_xattn.partition_broadcast(P)).then_inc(weights_in, 16)
            sp.dma_start(wp[:, :, :], W["Wp"].rearrange("(k p) c -> p k c", p=P)).then_inc(weights_in, 16)
            load_xr(0)
            sp.dma_start(wr[:, :, :], router_w.rearrange("(k p) e -> p k e", p=P)).then_inc(route_loaded, 16)
            for t in range(QT):
                sp.dma_start(rb[:, t, :], router_bias.partition_broadcast(P)).then_inc(route_loaded, 16)
            sp.dma_start(gate2[:, :], g_ffn.partition_broadcast(P)).then_inc(route_loaded, 16)
            sp.wait_ge(route_vec, 1)
            sp.dma_start(lists.rearrange("(p n) a -> p (n a)", p=P), zeros[:, :]).then_inc(lists_zeroed, 16)

            def body(kind, b, two_ahead=True):
                prev, cur, nxt = PARTS[kind]
                if cur:
                    max_rows(kind, b, 0)
                if nxt and two_ahead:
                    sp.wait_ge(xn_ready, LN.upto(kind, b, 0))
                    load_x(1 if kind == "pro" else b + 2)
                elif nxt:
                    sp.wait_ge(xn_ready, LN.upto(kind, b, 0))
                    load_x(B - 1)
                if nxt and two_ahead:
                    sp.wait_ge(scalar_filled, SU.upto(kind, b, ("xT", QT - 1)))
                    load_ctx(1 if kind == "pro" else b + 2)
                if prev:
                    sp.wait_ge(vector_drained, VU.upto(kind, b, ("wp", QT - 1)))
                    sp.dma_start(x1s[b - 1].rearrange("(t p) c -> p t c", p=P), xr[:, :, :]).then_inc(x1_stored, 16)
                if nxt:
                    write_parts(kind, b, 0)
                    read_stack(kind, b, 0)
                if prev:
                    sp.wait_ge(xn2_ready, b)
                    sp.dma_start(xn_rows.rearrange("(b t p) c -> b p t c", p=P, t=QT)[b - 1],
                                 xn2[:, :, :]).then_inc(xn2_saved, 16)
                if cur:
                    max_rows(kind, b, 1)
                if prev:
                    sp.wait_ge(x1_stored, b * 16)
                    sp.wait_ge(xn2_saved, b * 16)
                    if cur:
                        load_xr(b)
                if nxt:
                    write_parts(kind, b, 1)
                    read_stack(kind, b, 1)

            body("pro", 0)
            body("first", 0)
            with sp.Fori(1, B - 2) as b:
                body("mid", b)
            body("mid", B - 2, two_ahead=False)
            body("last", B - 1)
            body("post", B)

        @block.gpsimd
        def _(pool):
            pool.memset(half[:, :], -0.5).then_inc(setup_pool, 1)
            pool.memset(ident[:, :], 0.0).then_inc(setup_pool, 1)
            pool.memset(tri[:, :, :], 0.0).then_inc(setup_pool, 1)
            pool.wait_ge(setup_pool, 3)
            pool.affine_select(out=ident[:, :], in_=ident[:, :], compare_op=ALU.not_equal, fill=1.0, base=0,
                               pattern=[[-1, P]], channel_multiplier=1).then_inc(setup_pool, 1)
            pool.affine_select(out=tri[:, :, :], in_=tri[:, :, :], compare_op=ALU.is_ge, fill=-BIG, base=0,
                               pattern=[[0, 4], [-1, P]], channel_multiplier=1).then_inc(setup_pool, 1)
            pool.wait_ge(setup_pool, 5)
            pool.tensor_copy(ident_b[:, :], ident[:, :]).then_inc(setup_pool, 1)
            pool.memset(vst[:, :, :, :, :], 0.0).then_inc(setup_pool, 1)
            pool.memset(vcst[:, :, :, :], 0.0).then_inc(setup_pool, 1)
            for c in range(KC):
                pool.wait_ge(setup_pool, 8 + c)
                pool.memset(stack[c][96:128, :, K0:ALLC], 1.0).then_inc(setup_pool, 1)
            pool.wait_ge(setup_pool, 10)
            pool.memset(vst[:, :, :, :, D:D + 1], 1.0).then_inc(setup_pool, 1)
            pool.memset(vcst[0:TC, :, :, D:D + 1], 1.0).then_inc(setup_pool, 1)
            pool.wait_ge(setup_pool, 12)
            pool.memset(vcst[TC:P, :, :, 32 + D:33 + D], 1.0).then_inc(setup_pool, 1)

            pool.wait_ge(setup_pool, 13)
            pool.memset(before[:, :], 1.0).then_inc(route_pool, 1)
            pool.memset(ones[:, :], 1.0).then_inc(route_pool, 1)
            pool.iota(iota_i[:, :, :], pattern=[[0, QT], [1, E]], base=0, channel_multiplier=0).then_inc(route_pool, 1)
            pool.iota(tok_i[:, :], pattern=[[P, QT]], base=0, channel_multiplier=1).then_inc(route_pool, 1)
            pool.iota(slot_i[:, :], pattern=[[P, 2 * QT]], base=E * N, channel_multiplier=1).then_inc(route_pool, 1)
            pool.iota(keep["starts"][:, :], pattern=[[N, E]], base=0, channel_multiplier=0,
                      allow_small_or_imprecise_dtypes=True).then_inc(route_pool, 1)
            pool.wait_ge(route_pool, 6)
            pool.affine_select(out=before[:, :], in_=before[:, :], compare_op=ALU.is_gt, fill=0.0, base=0,
                               pattern=[[1, P]], channel_multiplier=-1).then_inc(route_pool, 1)

            SCATTERS = {(0, 0): (2, 3), (0, 1): (4, 5), (1, 0): (6, 7), (1, 1): (0, 1)}

            def route_rstd(b):
                pool.wait_ge(mv2_ready, b)
                pool.sem_inc(passed, 1)
                pool.tensor_scalar(rstd2[:, :], mv2[:, :, 1], EPS, None, ALU.add).then_inc(rstd2_step, 1)
                pool.wait_ge(rstd2_step, b)
                pool.tensor_tensor(rstd2[:, :], rstd2[:, :], half[:, :], ALU.pow).then_inc(rstd2_ready, 1)

            def scatter(b, i):
                if i == 0:
                    pool.wait_ge(slot_ready, b)
                    pool.sem_inc(passed, 1)
                pool.indirect_dma_start(
                    out=lists[:, :], out_offset=bass.IndirectOffsetOnAxis(ap=slot[:, i:i + 1], axis=0),
                    in_=tokens[:, i % QT:i % QT + 1], in_offset=None).then_inc(scattered, 16)

            def rstd_of(n):
                pool.wait_ge(mv_ready, n)
                pool.sem_inc(passed, 1)
                pool.tensor_scalar(rstd[:, :], mv[:, :, 1], EPS, None, ALU.add).then_inc(rstd_step, 1)
                pool.wait_ge(rstd_step, n)
                pool.tensor_tensor(rstd[:, :], rstd[:, :], half[:, :], ALU.pow).then_inc(rstd_ready, 1)

            def split_max(kind, b, c):
                n = MSPLIT.upto(kind, b, c)
                pool.wait_ge(vector_drained, VU.start(kind, b) if c == 0 else VU.upto(kind, b, ("sm", 1, NSM - 1)))
                if c == 1:
                    pool.wait_ge(vector_filled, VU.upto(kind, b, ("mT", 0)))
                pool.sem_inc(passed, 1)
                src = nmax[c][:, :, :, :].rearrange("p q h s -> p q (h s)")
                h, m, l = (mparts[:, :, i, :] for i in range(3))
                pool.tensor_copy(h, src).then_inc(msplit_step, 1)
                pool.wait_ge(msplit_step, 3 * n - 2)
                pool.tensor_tensor(mres[:, :, :], src, h, ALU.subtract).then_inc(msplit_step, 1)
                pool.wait_ge(msplit_step, 3 * n - 1)
                pool.sem_inc(passed, 1)
                pool.tensor_copy(m, mres[:, :, :]).then_inc(msplit_step, 1)
                pool.wait_ge(msplit_step, 3 * n)
                pool.tensor_tensor(l, mres[:, :, :], m, ALU.subtract).then_inc(msplit_done, 1)

            def mask_group(kind, b, c, g):
                for k, name in enumerate(GROUP):
                    if k == 7 and (c, g) == (1, 1) and PARTS[kind][2]:
                        rstd_of(LN.upto(kind, b, 0) + 1)
                    if k in (3, 4, 5) and PARTS[kind][0]:
                        for i in SCATTERS.get((c, g), ())[k - 3:k - 2]:
                            scatter(b, i)
                    if name[0] == "X":
                        continue
                    s = PT_SLOT[name]
                    pool.wait_ge(scalar_drained, SU.upto(kind, b, ("st", c, len(GROUP) * g + k)))
                    pool.sem_inc(passed, 1)
                    if name[0] == "A":
                        v, pat = pt[g][:, s, 0:P], [[1, P]]
                    else:
                        step = {"B": 3 * P, "C": 2 * P}[name[0]]
                        v = pt[g][:, s, 0:512].rearrange("p (a k) -> p a k", k=P)[:, 0:4:step // P, :]
                        pat = [[0, 2], [1, P]]
                    pool.affine_select(out=v, in_=v, compare_op=ALU.is_ge, fill=0.0, base=0, pattern=pat,
                                       channel_multiplier=-1).then_inc(masked, 1)

            def add_cross(kind, b, c, g):
                pool.wait_ge(vector_drained, VU.upto(kind, b, ("tU", c, g, "s")))
                h = HU * c + HEAD_GROUP * g
                dst = y[:, :, h:h + HEAD_GROUP, :]
                pool.tensor_tensor(dst, dst, yc[g][:, :, :, :], ALU.add).then_inc(y_added, 1)

            def body(kind, b):
                prev, cur, nxt = PARTS[kind]
                for c in range(KC):
                    if cur:
                        split_max(kind, b, c)
                    if kind == "pro" and c == 0:
                        rstd_of(1)
                    if prev and c == 0:
                        add_cross(kind, b, 1, 1)
                        pool.wait_ge(xr_in, b * 16)
                        for t in range(QT):
                            last = pool.tensor_tensor(xr[:, t, :], xr[:, t, :], bpg[:, :], ALU.add)
                        last.then_inc(xres_ready, 1)
                    if cur and c == 1:
                        add_cross(kind, b, 0, 1)
                    if prev and c == 0:
                        route_rstd(b)
                    if cur:
                        mask_group(kind, b, c, 0)
                    if nxt:
                        pool.wait_ge(m_ready, 4 * SPLIT.upto(kind, b, c))
                        pool.tensor_tensor(parts[:, 2, :], q32[:, :], parts[:, 1, :], ALU.subtract).then_inc(split_done, 1)
                    if nxt and not cur and c == 1:
                        rstd_of(LN.upto(kind, b, 0) + 1)
                    if cur:
                        mask_group(kind, b, c, 1)
                        add_cross(kind, b, c, 0)
                    elif prev:
                        for g in range(2):
                            for i in SCATTERS.get((c, g), ()):
                                scatter(b, i)

            pool.wait_ge(setup_vec, 7)
            pool.wait_ge(y_added, 4)
            pool.wait_ge(route_vec, 6)
            pool.wait_ge(lists_zeroed, 16)
            over_batches(pool, body)
            for i in range(2, 2 * QT):
                scatter(B, i)
            pool.wait_ge(scattered, 16 * (2 * QT * B + 2 * QT - 2))

        @block.scalar
        def _(act):
            act.wait_ge(weights_in, 16 * NW)
            act.activation(gate[:, :], gate[:, :], ACT.Tanh).then_inc(gate_ready, 1)
            act.wait_ge(route_loaded, 16 * ROUTE_LOADS)
            act.activation(gate2[:, :], gate2[:, :], ACT.Tanh).then_inc(gate2_ready, 1)
            act.wait_ge(setup_vec, 7)

            def bank(kind, name):
                return banks_s[SU.slot(kind, name, RING)]

            def transposed(kind, b):
                for t in range(QT):
                    act.wait_ge(scalar_filled, SU.upto(kind, b, ("xT", t)))
                    ps = bank(kind, ("xT", t))
                    if t == QT - 1:
                        act.activation(ctxT[:, :], ps[:, KC * P:(KC + 1) * P], ACT.Copy)
                    src = ps[:, 0:KC * P].rearrange("p (k t) -> p k t", k=KC)
                    act.activation(xnT[:, :, t * P:(t + 1) * P], src, ACT.Copy).then_inc(scalar_drained, 1)

            def projected(kind, b, c):
                n = SPLIT.upto(kind, b, c)
                if n > 1 if kind == "pro" else True:
                    act.wait_ge(split_done, n - 1)
                if n > 1 if kind == "pro" else True:
                    act.wait_ge(scr_written, 16 * (n - 1))
                for i, cols in enumerate(COLS):
                    act.wait_ge(scalar_filled, SU.upto(kind, b, ("proj", c, i)))
                    act.activation(q32[:, cols], bank(kind, ("proj", c, i))[:, 0:cols.stop - cols.start], ACT.Identity,
                                   bias=bias[:, 2 * i + c:2 * i + c + 1]).then_inc(scalar_drained, 1)
                    act.wait_ge(scalar_drained, SU.upto(kind, b, ("proj", c, i)))
                    act.activation(parts[:, 0, cols], q32[:, cols], ACT.Copy).then_inc(h_ready, 1)
                    if i in (1, 2):
                        middle_part(kind, b, c, i - 1)

            def middle_part(kind, b, c, i):
                act.wait_ge(r_ready, 4 * SPLIT.upto(kind, b, c) - 3 + i)
                act.activation(parts[:, 1, COLS[i]], q32[:, COLS[i]], ACT.Copy).then_inc(m_ready, 1)

            def unnormalised(kind, b, w, c, g):
                if c == 1:
                    act.wait_ge(vector_filled, VU.upto(kind, b, ("tU", 0, g, w)))
                elif g == 0:
                    act.wait_ge(vector_filled, VU.start(kind, b))
                elif PARTS[kind][0]:
                    act.wait_ge(vector_filled, VU.upto(kind, b, ("tU", 1, 1, w)))
                act.wait_ge(pv_filled, PV.upto(kind, b, (w, c, g)))
                act.activation(usum[w, g][:, :], (pv_cross if w == "x" else pv_self)[:, :], ACT.Copy).then_inc(pv_drained, 1)

            def route_exp(b):
                act.wait_ge(logits_shifted, b)
                act.activation(prob[:, :, :], logit[:, :, :], ACT.Exp).then_inc(logits_exp, 1)

            def exponentials(kind, b, c, k):
                g, name = k // len(GROUP), GROUP[k % len(GROUP)]
                if k % len(GROUP) == 0:
                    act.wait_ge(pv_filled, PV.upto(kind, b, ("s", c, g)) - 4)
                act.wait_ge(scalar_filled, SU.upto(kind, b, ("st", c, k)))
                dst = ct[g][:, name[1], :] if name[0] == "X" else pt[g][:, PT_SLOT[name], :]
                act.activation(dst, bank(kind, ("st", c, k))[:, :], ACT.Exp, scale=SCALE).then_inc(scalar_drained, 1)

            def body(kind, b):
                prev, cur, nxt = PARTS[kind]
                for c in range(KC):
                    if nxt and c == 0:
                        transposed(kind, b)
                    if nxt:
                        projected(kind, b, c)
                    if cur:
                        for k in range(NST):
                            exponentials(kind, b, c, k)
                            if nxt and k < 2:
                                middle_part(kind, b, c, 2 + k)
                            if k == ROUTE_EXP and prev and c == 0:
                                route_exp(b)
                            if k == 18:
                                unnormalised(kind, b, "x", c, 0)
                        unnormalised(kind, b, "s", c, 0)
                        unnormalised(kind, b, "x", c, 1)
                        unnormalised(kind, b, "s", c, 1)
                    elif nxt:
                        for i in (2, 3):
                            middle_part(kind, b, c, i)
                    elif c == 0:
                        route_exp(b)

            over_batches(act, body)

        @block.vector
        def _(dve):
            dve.memset(zeros[:, :], 0).then_inc(route_vec, 1)
            dve.wait_ge(weights_in, 16 * NW)
            for i, n in enumerate(("q", "cq", "k")):
                dve.tensor_copy(wq[n][:, :, :, :].rearrange("p k c (d h) -> p (k c) d h", h=HU),
                                raw[n].rearrange("p k (c h d) -> p (k c) d h", c=KC, d=D)).then_inc(setup_vec, 1)
            dve.tensor_copy(wck[:, :, :].rearrange("p c (d h) -> p c d h", h=HU),
                            raw_ck.rearrange("p (c h d) -> p c d h", c=KC, d=D)).then_inc(setup_vec, 1)
            dve.tensor_copy(bias_perm[:, :].rearrange("r (d h) -> r d h", h=HU),
                            bias_rows[:, :].rearrange("r (h d) -> r d h", d=D)).then_inc(setup_vec, 1)
            dve.wait_ge(gate_ready, 1)
            dve.tensor_scalar(wp[:, :, :], wp[:, :, :], gate[:, 0:1], None, ALU.mult).then_inc(setup_vec, 1)
            dve.tensor_scalar(bpg[:, :], bpg[:, :], gate[:, 0:1], None, ALU.mult).then_inc(y_added, 4)
            dve.wait_ge(setup_pe, 1)
            dve.tensor_copy(bias[:, :], banks_v[0][:, 0:8]).then_inc(setup_vec, 1)
            dve.memset(recip["x"][:, :, :], 1.0).then_inc(pv_filled, 8)
            dve.memset(mres[:, :, :], 0.0).then_inc(pv_drained, 8)
            dve.wait_ge(pv_filled, 8)
            dve.wait_ge(setup_pool, 13)
            dve.wait_ge(route_pool, 7)
            dve.wait_ge(gate2_ready, 1)
            dve.tensor_copy(iota[:, :, :], iota_i[:, :, :]).then_inc(route_vec, 1)
            dve.tensor_copy(tok[:, :], tok_i[:, :]).then_inc(route_vec, 1)
            dve.tensor_copy(running[:, :], keep["starts"][:, :]).then_inc(route_vec, 1)
            dve.memset(tokens[:, :], 0).then_inc(route_vec, 1)
            dve.tensor_copy(slot[:, :], slot_i[:, :]).then_inc(route_vec, 1)
            dve.wait_ge(route_vec, 6)

            def bank(kind, name):
                return banks_v[VU.slot(kind, name, RING)]

            def filled(kind, b, name):
                dve.wait_ge(vector_filled, VU.upto(kind, b, name))
                return bank(kind, name)

            def ln_stats(n):
                dve.wait_ge(x_in, 16 * n)
                for t in range(QT):
                    last = dve.bn_stats(stats[:, t, :], xt[:, t, :])
                last.then_inc(stats_ready, 1)
                dve.wait_ge(stats_ready, n)
                dve.sem_inc(passed, 1)
                if not isinstance(n, int) or n > 1:
                    dve.wait_ge(xn_ready, n - 1)
                    dve.sem_inc(passed, 1)
                for t in range(QT):
                    last = dve.bn_aggr(mv[:, t, :], stats[:, t, :])
                last.then_inc(mv_ready, 1)

            def ln_apply(n):
                dve.wait_ge(rstd_ready, n)
                for t in range(QT):
                    last = dve.tensor_scalar(xn[:, t, :], xt[:, t, :], mv[:, t, 0:1], rstd[:, t:t + 1],
                                             ALU.subtract, ALU.mult)
                last.then_inc(xn_ready, 1)

            def values(kind, b, c):
                if kind != "pro":
                    dve.wait_ge(pv_filled, PV.start(kind, b) if c == 1 else PV.upto(kind, b, ("s", 0, 1)))
                ps = filled(kind, b, ("v", c))
                dve.tensor_tensor(vst[:, :, c, :, 0:D], ps[:, :].rearrange("p (t h d) -> p t h d", t=QT, d=D),
                                  bv[:, c, :, :].rearrange("p t (h d) -> p t h d", d=D), ALU.add).then_inc(vector_drained, 1)
                ps = filled(kind, b, ("vc", c))
                for half_, col in ((0, 0), (1, 32)):
                    rows = slice(half_ * TC, (half_ + 1) * TC)
                    last = dve.tensor_tensor(
                        vcst[rows, c, :, col:col + D],
                        ps[rows, 0:P].rearrange("p (a i d) -> p a i d", i=2, d=D)[:, :, half_, :],
                        bcv[rows, c * P:(c + 1) * P].rearrange("p (a i d) -> p a i d", i=2, d=D)[:, :, half_, :], ALU.add)
                last.then_inc(vector_drained, 1)

            CHAIN = 18
            chained = [0]

            def link(ins):
                chained[0] += 1
                ins.then_inc(route_step, 1)

            def linked(b):
                dve.wait_ge(route_step, (b - 1) * CHAIN + chained[0])

            def route_step_of(kind, b, what):
                bc = [P, QT, E]
                if what == "stats":
                    chained[0] = 0
                    dve.wait_ge(vector_drained, VU.upto(kind, b, ("wp", QT - 1)))
                    for t in range(QT):
                        last = dve.bn_stats(stats2[:, t, :], xr[:, t, :])
                    last.then_inc(stats2_ready, 1)
                elif what == "aggregate":
                    dve.wait_ge(stats2_ready, b)
                    dve.sem_inc(passed, 1)
                    for t in range(QT):
                        last = dve.bn_aggr(mv2[:, t, :], stats2[:, t, :])
                    last.then_inc(mv2_ready, 1)
                elif what == "normalise":
                    dve.wait_ge(rstd2_ready, b)
                    for t in range(QT):
                        last = dve.tensor_scalar(xn2[:, t, :], xr[:, t, :], mv2[:, t, 0:1], rstd2[:, t:t + 1],
                                                 ALU.subtract, ALU.mult)
                    last.then_inc(xn2_ready, 1)
                elif what[0] == "rT":
                    t = what[1]
                    ps = filled(kind, b, what)
                    dve.tensor_copy(xT2[:, :, t * P:(t + 1) * P],
                                    ps[:, 0:KC * P].rearrange("p (k t) -> p k t", k=KC)).then_inc(vector_drained, 1)
                elif what[0] == "rl":
                    ps = filled(kind, b, what)
                    dve.tensor_tensor(logit[:, :, :], ps[:, 0:QT * E].rearrange("p (t e) -> p t e", e=E), rb[:, :, :],
                                      ALU.add).then_inc(vector_drained, 1)
                elif what == "max":
                    dve.wait_ge(vector_drained, VU.upto(kind, b, ("rl",)))
                    link(dve.tensor_reduce(m4[:, :], logit[:, :, :], axis=AX, op=ALU.max))
                elif what == "shift":
                    linked(b)
                    dve.tensor_tensor(logit[:, :, :], logit[:, :, :], m4[:, :].unsqueeze(2).to_broadcast(bc),
                                      ALU.subtract).then_inc(logits_shifted, 1)
                elif what == "sum":
                    dve.wait_ge(logits_exp, b)
                    link(dve.tensor_reduce(z4[:, :], prob[:, :, :], axis=AX, op=ALU.add))
                elif what == "invert":
                    linked(b)
                    link(dve.reciprocal(z4[:, :], z4[:, :]))
                elif what == "probs":
                    linked(b)
                    link(dve.tensor_tensor(prob[:, :, :], prob[:, :, :], z4[:, :].unsqueeze(2).to_broadcast(bc), ALU.mult))
                elif what == "top":
                    linked(b)
                    dve.sem_inc(passed, 1)
                    for t in range(QT):
                        last = dve.max(top[:, t, :], prob[:, t, :])
                    link(last)
                elif what == "index":
                    linked(b)
                    dve.sem_inc(passed, 1)
                    for t in range(QT):
                        last = dve.max_index(topi[:, t, :], top[:, t, :], prob[:, t, :])
                    link(last)
                elif what == "as float":
                    linked(b)
                    dve.tensor_tensor(s4[:, :], top[:, :, 0], top[:, :, 1], ALU.add)
                    link(dve.tensor_copy(topf[:, :, :], topi[:, :, 0:2]))
                elif what == "hot":
                    linked(b)
                    dve.tensor_scalar(s4[:, :], s4[:, :], 1e-6, None, ALU.add)
                    for k in range(2):
                        last = dve.tensor_tensor(hot[k][:, :, :], iota[:, :, :],
                                                 topf[:, :, k].unsqueeze(2).to_broadcast(bc), ALU.is_equal)
                    link(last)
                elif what == "both":
                    linked(b)
                    dve.tensor_tensor(both[:, :, :], hot[0][:, :, :], hot[1][:, :, :], ALU.add).then_inc(hot_ready, 1)
                    dve.tensor_scalar(wid2[:, :, :], topf[:, :, :], float(E - 1), gate2[:, 0:1], ALU.is_equal, ALU.mult)
                    link(dve.reciprocal(s4[:, :], s4[:, :]))
                elif what == "weigh":
                    linked(b)
                    link(dve.tensor_tensor(w2[:, :, :], top[:, :, 0:2], s4[:, :].unsqueeze(2).to_broadcast([P, QT, 2]),
                                           ALU.mult))
                elif what[0] == "rk":
                    ps = filled(kind, b, what)
                    link(dve.tensor_tensor(place[:, :, :], ps[:, 0:QT * E].rearrange("p (t e) -> p t e", e=E),
                                           running[:, :].unsqueeze(1).to_broadcast(bc), ALU.add))
                    linked(b)
                    dve.tensor_tensor(running[:, :], running[:, :], ps[:, QT * E:(QT + 1) * E],
                                      ALU.add).then_inc(vector_drained, 1)
                elif what == "identity":
                    linked(b)
                    link(dve.tensor_tensor(wid2[:, :, :], w2[:, :, :], wid2[:, :, :], ALU.mult))
                elif what == "weights":
                    linked(b)
                    link(dve.tensor_reduce(keep["identity"][:, bass.ds((b - 1) * QT, QT)], wid2[:, :, :], axis=AX,
                                           op=ALU.add))
                    link(dve.scalar_tensor_tensor(out=keep["weight"][:, bass.ds((b - 1) * QT, QT), :], in0=w2[:, :, :],
                                                  scalar=gate2[:, 0:1], in1=wid2[:, :, :], op0=ALU.mult,
                                                  op1=ALU.subtract))
                elif what == "at":
                    dve.wait_ge(vector_drained, VU.upto(kind, b, ("rk",)))
                    for k in range(2):
                        link(dve.tensor_tensor(hot[k][:, :, :], hot[k][:, :, :], place[:, :, :], ALU.mult))
                elif what == "slots":
                    linked(b)
                    for k in range(2):
                        last = dve.tensor_reduce(slotf[:, k, :], hot[k][:, :, :], axis=AX, op=ALU.add)
                    link(last)
                    dve.wait_ge(scattered, 16 * (2 * QT * b - 2))
                    link(dve.tensor_copy(tokens[:, :], tok[:, :]))
                    assert chained[0] == CHAIN, chained
                else:
                    linked(b)
                    dve.tensor_scalar(tok[:, :], tok[:, :], float(T), None, ALU.add)
                    dve.tensor_copy(keep["row"][:, bass.ds((b - 1) * 2, 2), :], slotf[:, :, :])
                    dve.tensor_copy(slot[:, :], slotf[:, :, :].rearrange("p k t -> p (k t)")).then_inc(slot_ready, 1)

            def subtract_part(kind, b, c, i):
                dve.wait_ge(h_ready, 4 * SPLIT.upto(kind, b, c) - 3 + i)
                dve.tensor_tensor(q32[:, COLS[i]], q32[:, COLS[i]], parts[:, 0, COLS[i]], ALU.subtract).then_inc(r_ready, 1)

            def maxima_and_route(kind, b, c, other, work):
                for k in range(NST):
                    if PARTS[kind][2] and (c, k) == LN_SUMS:
                        ln_stats(LN.upto(kind, b, 0) + 1)
                    if PARTS[kind][2] and (c, k) == LN_ROWS:
                        dve.wait_ge(scalar_filled, SU.upto(kind, b, ("xT", QT - 1)))
                        ln_apply(LN.upto(kind, b, 0) + 1)
                    if work:
                        maxima(kind, b, other, BESIDE[k])
                    if PARTS[kind][0]:
                        for table in (ROUTE_UNITS, ROUTE_STEPS):
                            if (c, k) in table:
                                route_step_of(kind, b, table[c, k])

            def maxima(kind, b, c, ks):
                for k in ks:
                    what, qt, h, n = MAXU[k]
                    ps = filled(kind, b, ("sm", c, k))
                    if what == "cross":
                        src, dst = ps[:, :].rearrange("p (h t) -> p h t", t=TC), nmax[c][:, qt, :, 1]
                    else:
                        w = (qt + 1) * P
                        src = ps[:, 0:n * w].rearrange("p (h t) -> p h t", t=w)
                        dst = nmax[c][:, qt, h:h + n, 0]
                    dve.tensor_reduce(dst, src, axis=AX, op=ALU.max, negate=True).then_inc(vector_drained, 1)

            def max_transposed(kind, b, c):
                ps = filled(kind, b, ("mT", c))
                dve.tensor_copy(mT[c][:, :], ps[:, :].bitcast(BF16)[0:3 * HU * 2, 0:T]).then_inc(vector_drained, 1)

            def normalise(kind, b, c, g):
                n = 2 * YADD.upto(kind, b, (c, g)) - 2 * YADD.credit
                h = HU * c + HEAD_GROUP * g
                for w, dst in (("x", yc[g][:, :, :, :]), ("s", y[:, :, h:h + HEAD_GROUP, :])):
                    if w == "x":
                        dve.wait_ge(y_added, YADD.upto(kind, b, (c, g)) - 2)
                    ps = filled(kind, b, ("tU", c, g, w))[:, :].rearrange("p (t j r) -> p t j r", t=QT, r=32)
                    dve.reciprocal(recip[w][:, :, :], ps[:, :, :, D]).then_inc(norm_step, 1)
                    dve.wait_ge(norm_step, n - 1 if w == "x" else n)
                    dve.tensor_tensor(dst, ps[:, :, :, 0:D], recip[w][:, :, :].unsqueeze(3).to_broadcast([P, QT, HEAD_GROUP, D]),
                                      ALU.mult).then_inc(vector_drained, 1)

            def output_transposed(kind, b):
                for k in range(KC):
                    ps = filled(kind, b, ("yT", k))
                    dve.tensor_copy(yT[:, k, :], ps[:, :]).then_inc(vector_drained, 1)

            def output_rows(kind, b):
                dve.wait_ge(xres_ready, b)
                for t in range(QT):
                    ps = filled(kind, b, ("wp", t))
                    dve.tensor_tensor(xr[:, t, :], ps[:, 0:C], xr[:, t, :], ALU.add).then_inc(vector_drained, 1)

            def body(kind, b):
                prev, cur, nxt = PARTS[kind]
                if cur:
                    values(kind, b, 1)
                if kind == "pro":
                    ln_stats(1)
                if prev:
                    normalise(kind, b, 1, 1)
                if kind == "pro":
                    ln_apply(1)
                if cur:
                    max_transposed(kind, b, 0)
                    maxima(kind, b, 1, range(2))
                if nxt:
                    subtract_part(kind, b, 0, 0)
                if prev:
                    output_transposed(kind, b)
                for i in (1, 2):
                    if cur:
                        maxima(kind, b, 1, (2 * i, 2 * i + 1))
                    if nxt:
                        subtract_part(kind, b, 0, i)
                if nxt:
                    subtract_part(kind, b, 0, 3)
                if prev:
                    output_rows(kind, b)
                for c in range(KC):
                    other = 1 - c
                    if c == 1:
                        if nxt:
                            values(kind, b, 0)
                        if cur:
                            normalise(kind, b, 0, 1)
                            max_transposed(kind, b, 1)
                        if nxt:
                            for i in range(4):
                                if i < 3:
                                    maxima(kind, b, 0, (2 * i, 2 * i + 1))
                                subtract_part(kind, b, 1, i)
                    work = cur if c == 0 else nxt
                    maxima_and_route(kind, b, c, other, work)
                    if cur:
                        normalise(kind, b, c, 0)
                    if work:
                        maxima(kind, b, other, range(SM_MID, NSM))

            over_batches(dve, body)
            dve.wait_ge(slot_ready, B)
            dve.tensor_copy(keep["counts"][:, :], running[:, :]).then_inc(route_vec, 1)
            dve.wait_ge(route_vec, 7)

        @block.tensor
        def _(pe):
            pe.wait_ge(setup_pool, 13)
            pe.wait_ge(setup_vec, 5)
            pe.transpose(banks_v[0][:, 0:8], bias_perm[:, :], ident[0:8, 0:8]).then_inc(setup_pe, 1)
            pe.wait_ge(setup_vec, 7)
            pe.wait_ge(y_added, 4)
            pe.wait_ge(route_pool, 7)

            def claim_s(kind, b, name):
                n = SU.upto(kind, b, name) - RING
                if kind != "pro" or n > 0:
                    pe.wait_ge(scalar_drained, n)
                return banks_s[SU.slot(kind, name, RING)]

            def claim_v(kind, b, name):
                n = VU.upto(kind, b, name) - RING
                if kind != "pro" or n > 0:
                    pe.wait_ge(vector_drained, n)
                return banks_v[VU.slot(kind, name, RING)]

            def value_products(kind, b, c):
                ps = claim_v(kind, b, ("v", c))
                for t in range(QT):
                    for k in range(KC):
                        last = pe.matmul(ps[:, t * P:(t + 1) * P], xnT[:, k, t * P:(t + 1) * P],
                                         wv[:, k, c * P:(c + 1) * P], start=(k == 0), stop=(k == KC - 1))
                last.then_inc(vector_filled, 1)
                ps = claim_v(kind, b, ("vc", c))
                pe.matmul(ps[:, 0:P], ctxT[:, :], wcv[:, c * P:(c + 1) * P], start=True, stop=True).then_inc(vector_filled, 1)

            def transpose_max(kind, b, c):
                ps = claim_v(kind, b, ("mT", c))
                pe.wait_ge(msplit_done, MSPLIT.upto(kind, b, c))
                pe.sem_inc(passed, 1)
                for q in range(QT):
                    last = pe.transpose(ps[:, :].bitcast(BF16)[0:3 * HU * 2, q * P:(q + 1) * P],
                                        mparts[:, q, :, :].rearrange("p s h -> p (s h)"), ident_b[:, :])
                last.then_inc(vector_filled, 1)

            def transpose_inputs(kind, b):
                pe.wait_ge(xn_ready, LN.upto(kind, b, 0))
                pe.wait_ge(ctx_in, 32 * LN.upto(kind, b, 0))
                for t in range(QT):
                    ps = claim_s(kind, b, ("xT", t))
                    if t == QT - 1:
                        pe.transpose(ps[:, KC * P:(KC + 1) * P], ctile[:, :], ident[:, :])
                    for k in range(KC):
                        last = pe.transpose(ps[:, k * P:(k + 1) * P], xn[:, t, k * P:(k + 1) * P], ident[:, :])
                    last.then_inc(scalar_filled, 1)

            def transpose_sums(kind, b, c, g):
                for w in ("x", "s"):
                    ps = claim_v(kind, b, ("tU", c, g, w))
                    pe.wait_ge(pv_drained, PV.upto(kind, b, (w, c, g)) if PARTS[kind][1] and not (c, g) == (1, 1)
                               else PV.start(kind, b))
                    for t in range(QT):
                        last = pe.transpose(ps[:, t * P:(t + 1) * P], usum[w, g][:, t * P:(t + 1) * P], ident[:, :])
                    last.then_inc(vector_filled, 1)

            def projections(kind, b, c, which):
                for i in which:
                    ps = claim_s(kind, b, ("proj", c, i))
                    if i == 3:
                        pe.matmul(ps[:, 0:TC], wck[:, c, :], ctxT[:, 0:TC], start=True, stop=True).then_inc(scalar_filled, 1)
                        continue
                    for k in range(KC):
                        last = pe.matmul(ps[:, :], wq[("q", "cq", "k")[i]][:, k, c, :], xnT[:, k, :],
                                         start=(k == 0), stop=(k == KC - 1))
                    last.then_inc(scalar_filled, 1)

            def score_unit(kind, b, c, k):
                g, (what, j) = k // len(GROUP), GROUP[k % len(GROUP)]
                ps = claim_s(kind, b, ("st", c, k))
                rows = STACK + MROWS

                def mm(out, head, key0, nk, q0, nq, **kw):
                    return pe.matmul(out, stack[c][0:rows, head, key0:key0 + nk], stack[c][0:rows, head, q0:q0 + nq],
                                     start=True, stop=True, **kw)

                h = HEAD_GROUP * g + j
                if what == "X":
                    h = HEAD_GROUP * g + 2 * j
                    for i in range(2):
                        last = mm(ps[i * TC:(i + 1) * TC, :], h + i, KC0, TC, CQ0, T)
                elif what == "A":
                    last = mm(ps[:, :], h, K0, P, Q0, T)
                elif what == "B":
                    mm(ps[:, 0:3 * P], h, K0 + P, P, Q0 + P, 3 * P)
                    last = mm(ps[:, 3 * P:], h, K0 + 3 * P, P, Q0 + 3 * P, P)
                else:
                    for i in range(2):
                        last = mm(ps[:, i * 2 * P:(i + 1) * 2 * P], h + i, K0 + 2 * P, P, Q0 + 2 * P, 2 * P)
                last.then_inc(scalar_filled, 1)

            def max_unit(kind, b, c, k):
                what, qt, h0, n = MAXU[k]
                ps = claim_v(kind, b, ("sm", c, k))
                if what == "cross":
                    for h in range(n):
                        last = pe.matmul(ps[:, h * TC:(h + 1) * TC], stack[c][0:STACK, h, CQ0 + qt * P:CQ0 + (qt + 1) * P],
                                         stack[c][0:STACK, h, KC0:KC0 + TC], start=True, stop=True)
                else:
                    w = (qt + 1) * P
                    pe.matmul(ps[:, 0:n * w].rearrange("p (h t) -> p h t", t=w)[:, :, qt * P:w], ident_b[:, :],
                              tri[:, 0:n, :], start=True, stop=False, skip_group_check=True)
                    for i in range(n):
                        last = pe.matmul(ps[:, i * w:(i + 1) * w], stack[c][0:STACK, h0 + i, qt * P:(qt + 1) * P],
                                         stack[c][0:STACK, h0 + i, K0:K0 + w], start=False, stop=(i == n - 1),
                                         skip_group_check=True)
                last.then_inc(vector_filled, 1)

            def pv_cross_products(kind, b, c, g):
                pe.wait_ge(pv_drained, PV.upto(kind, b, ("x", c, g)) - 2)
                pe.wait_ge(scalar_drained, SU.upto(kind, b, ("st", c, len(GROUP) * g + 1)))
                for jp in range(2):
                    last = pe.matmul(pv_cross[64 * jp:64 * jp + 64, :], vcst[:, c, 2 * g + jp, :], ct[g][:, jp, :],
                                     start=True, stop=True)
                last.then_inc(pv_filled, 1)

            def pv_self_products(kind, b, c, g, kt):
                if kt == 0:
                    pe.wait_ge(pv_drained, PV.upto(kind, b, ("s", c, g)) - 2)
                    pe.wait_ge(masked, MASKED.upto(kind, b, (c, g, 9)))
                for j in range(4):
                    if kt == 0:
                        src = pt[g][:, PT_SLOT[("A", j)], :]
                    elif kt == 1:
                        src = pt[g][:, PT_SLOT[("B", j)], 0:3 * P]
                    elif kt == 3:
                        src = pt[g][:, PT_SLOT[("B", j)], 3 * P:]
                    else:
                        src = pt[g][:, PT_SLOT[("C", j // 2 * 2)], (j % 2) * 2 * P:(j % 2 + 1) * 2 * P]
                    last = pe.matmul(pv_self[32 * j:32 * j + 32, kt * P:T], vst[:, kt, c, HEAD_GROUP * g + j, :], src,
                                     start=(kt == 0), stop=(kt == QT - 1), skip_group_check=True)
                if kt == QT - 1:
                    last.then_inc(pv_filled, 1)

            def route_unit(kind, b, name):
                ps = claim_v(kind, b, name)
                if name[0] == "rT":
                    t = name[1]
                    pe.wait_ge(xn2_ready, b)
                    for k in range(KC):
                        last = pe.transpose(ps[:, k * P:(k + 1) * P], xn2[:, t, k * P:(k + 1) * P], ident[:, :])
                elif name[0] == "rl":
                    pe.wait_ge(vector_drained, VU.upto(kind, b, ("rT", QT - 1)))
                    for t in range(QT):
                        for k in range(KC):
                            last = pe.matmul(ps[:, t * E:(t + 1) * E], xT2[:, k, t * P:(t + 1) * P], wr[:, k, :],
                                             start=(k == 0), stop=(k == KC - 1))
                else:
                    pe.wait_ge(hot_ready, b)
                    for t in range(QT + 1):
                        srcs = [(before, t)] if t < QT else []
                        srcs += [(ones, u) for u in range(t)]
                        for i, (m, u) in enumerate(srcs):
                            last = pe.matmul(ps[:, t * E:(t + 1) * E], m[:, :], both[:, u, :], start=(i == 0),
                                             stop=(i == len(srcs) - 1))
                last.then_inc(vector_filled, 1)

            def main(kind, b, c):
                prev, cur, nxt = PARTS[kind]
                work = cur if c == 0 else nxt
                other = 1 - c
                if cur:
                    pe.wait_ge(m_in[c], 16 * (b + 1))
                    pe.wait_ge(vector_drained, VU.start(kind, b))
                for k in range(NST):
                    if cur:
                        score_unit(kind, b, c, k)
                        if k == 14:
                            pv_cross_products(kind, b, c, 0)
                        if k in (16, 18, 20, 22):
                            pv_self_products(kind, b, c, 0, (k - 16) // 2)
                    if work:
                        for u in BESIDE[k]:
                            max_unit(kind, b, other, u)
                    if prev and (c, k) in ROUTE_UNITS:
                        route_unit(kind, b, ROUTE_UNITS[c, k])
                if cur:
                    pv_cross_products(kind, b, c, 1)
                    for kt in range(QT):
                        pv_self_products(kind, b, c, 1, kt)
                    transpose_sums(kind, b, c, 0)
                if work:
                    for k in range(SM_MID, NSM):
                        max_unit(kind, b, other, k)

            def transpose_output(kind, b):
                pe.wait_ge(y_added, YADD.upto(kind, b, (1, 1)))
                for k in range(KC):
                    ps = claim_v(kind, b, ("yT", k))
                    for t in range(QT):
                        last = pe.transpose(ps[:, t * P:(t + 1) * P],
                                            y[:, t, HU * k:HU * (k + 1), :].rearrange("p h d -> p (h d)"), ident[:, :])
                    last.then_inc(vector_filled, 1)

            def output_projection(kind, b):
                pe.wait_ge(vector_drained, VU.upto(kind, b, ("yT", KC - 1)))
                for t in range(QT):
                    ps = claim_v(kind, b, ("wp", t))
                    for k in range(KC):
                        last = pe.matmul(ps[:, 0:C], yT[:, k, t * P:(t + 1) * P], wp[:, k, :], start=(k == 0),
                                         stop=(k == KC - 1))
                    last.then_inc(vector_filled, 1)

            def body(kind, b):
                prev, cur, nxt = PARTS[kind]
                if cur:
                    value_products(kind, b, 1)
                if nxt:
                    transpose_inputs(kind, b)
                if prev:
                    transpose_sums(kind, b, 1, 1)
                if cur:
                    transpose_max(kind, b, 0)
                if nxt:
                    pe.wait_ge(scalar_drained, SU.upto(kind, b, ("xT", QT - 1)))
                    projections(kind, b, 0, (0,))
                if cur:
                    pe.wait_ge(stack_in[1], 16 * 7 * (b + 1))
                    for k in range(2):
                        max_unit(kind, b, 1, k)
                if prev:
                    transpose_output(kind, b)
                for i in (1, 2):
                    if nxt:
                        projections(kind, b, 0, (i,))
                    if cur:
                        for k in (2 * i, 2 * i + 1):
                            max_unit(kind, b, 1, k)
                if nxt:
                    projections(kind, b, 0, (3,))
                if prev:
                    output_projection(kind, b)
                main(kind, b, 0)
                if nxt:
                    value_products(kind, b, 0)
                if cur:
                    transpose_sums(kind, b, 0, 1)
                    transpose_max(kind, b, 1)
                if nxt:
                    for i in range(3):
                        projections(kind, b, 1, (i,))
                        if i == 0:
                            pe.wait_ge(stack_in[0], 16 * 7 * LN.upto(kind, b, 0))
                        for k in (2 * i, 2 * i + 1):
                            max_unit(kind, b, 0, k)
                    projections(kind, b, 1, (3,))
                main(kind, b, 1)

            over_batches(pe, body)


LANES = 8


def expert_tiles(N, ER):
    return (2 * N // P + ER + LANES) // LANES * LANES


def expert_phase(nc, W, sc, keep, N):
    ER, C, I = W["expert_gate_w"].shape
    E = ER + 1
    KC = C // P
    NT = expert_tiles(N, ER)
    xn_rows, lists, results = sc["xn_rows"], sc["lists"], sc["results"]

    with ExitStack() as st:
        def sb(name, shape, dt=F32):
            return st.enter_context(nc.sbuf_tensor(name, shape, dt))

        def ps(name):
            return st.enter_context(nc.psum_tensor(name, [P, 512], F32))

        def sem(name):
            return st.enter_context(nc.semaphore(name))

        passed = sem("passed_expert")
        ALLW = KC * 2 * I + C
        weights = sb("weights", [P, ER, ALLW])
        wgu = weights[:, :, 0:KC * 2 * I].rearrange("p e (k m i) -> p e k m i", k=KC, m=2)
        wd = weights[:, :, KC * 2 * I:]
        ident = sb("ident3", [P, P])
        tiles = sb("tiles", [P, E])
        tiles_i = sb("tiles_i", [P, E], I32)
        ends = [sb(f"ends{i}", [P, E]) for i in range(2)]
        num_i, num = sb("num_i", [1, NT], I32), sb("num", [1, NT])
        ge = sb("ge", [1, NT, ER])
        jump = sb("jump", [P, E])
        spare_row = sb("spare_row", [P, 1])
        row = keep["row"][:, :, :].rearrange("p b t -> p (b t)")
        ROWS = row.shape[1]
        past = sb("past", [P, ROWS, ER])
        back = sb("back", [P, ROWS])
        jumps = sb("jumps", [1, NT, ER])
        expert, offset = sb("expert", [1, NT]), sb("offset", [1, NT])
        NSTEP = NT + 4
        table = sb("table", [1, NSTEP, 4], I32)
        rows_i = sb("rows_i", [1, NT], I32)
        idx = [sb(f"idx{r}", [P, 1], I32) for r in range(LANES)]
        xg = [sb(f"xg{r}", [P, C]) for r in range(LANES)]
        xT = [sb(f"xTe{r}", [P, KC, P]) for r in range(2)]
        sg = [sb(f"sg{r}", [P, I]) for r in range(2)]
        hh = [sb(f"hh{r}", [P, I]) for r in range(2)]
        hT = [sb(f"hT{r}", [P, P]) for r in range(2)]
        yo = [sb(f"yo{r}", [P, C]) for r in range(LANES)]
        psX = [ps(f"psX{r}") for r in range(2)]
        psGU = [ps(f"psGU{r}") for r in range(2)]
        psH = [ps(f"psH{r}") for r in range(2)]
        psY = [ps(f"psY{r}") for r in range(2)]

        weights_in, pool_setup, table_step, table_ready = sem("c_weights"), sem("c_pool"), sem("table_step"), sem("table_ready")
        rows_ready = sem("rows_ready")
        idx_in = [sem(f"idx_in{r}") for r in range(LANES)]
        x_in = [sem(f"xg_in{r}") for r in range(LANES)]
        xT_filled, xT_drained = sem("cxT_filled"), sem("cxT_drained")
        gu_filled, silu_ready, h_ready = sem("cgu_filled"), sem("silu_ready"), sem("ch_ready")
        hT_filled, hT_drained = sem("hT_filled"), sem("hT_drained")
        y_filled, y_drained = sem("cy_filled"), sem("cy_drained")
        y_saved = [sem(f"cy_saved{r}") for r in range(LANES)]

        block = st.enter_context(nc.Block())

        @block.sync
        def _(sp):
            for k in range(KC):
                for m, n in enumerate(("expert_gate_w", "expert_up_w")):
                    sp.dma_start(wgu[:, :, k, m, :], W[n][:, k * P:(k + 1) * P, :].rearrange("e p i -> p e i")).then_inc(weights_in, 16)
            sp.dma_start(wd, W["expert_down_w"].rearrange("e i c -> i e c")).then_inc(weights_in, 16)
            sp.wait_ge(rows_ready, 1)
            sp.wait_ge(table_ready, 1)
            LAG = 2 * LANES

            def fetch(i, r, k):
                if not isinstance(k, int) or k > 0:
                    sp.wait_ge(x_in[r], 16 * k)
                row = sp.value_load(rows_i[0:1, bass.ds(i, 1)], min_val=0, max_val=ER * N)
                sp.dma_start(idx[r][:, :], lists[bass.ds(row, P), :]).then_inc(idx_in[r], 16)

            def save(i, r):
                sp.wait_ge(y_drained, i + 1)
                sp.dma_start(results.rearrange("(n p) c -> n p c", p=P)[i], yo[r][:, :]).then_inc(y_saved[r], 16)

            for k in range(2):
                for r in range(LANES):
                    fetch(k * LANES + r, r, k)
            with sp.Fori(2, NT // LANES) as k:
                for r in range(LANES):
                    save((k - 2) * LANES + r, r)
                    fetch(k * LANES + r, r, k)
            for i in range(NT - LAG, NT):
                save(i, i % LANES)
            for r in range(LANES):
                sp.wait_ge(y_saved[r], 16 * NT // LANES)

        @block.gpsimd
        def _(pool):
            pool.memset(ident[:, :], 0.0).then_inc(pool_setup, 1)
            pool.memset(table[:, :, :], 0).then_inc(pool_setup, 1)
            pool.iota(num_i[:, :], pattern=[[1, NT]], base=0, channel_multiplier=0).then_inc(pool_setup, 1)
            pool.iota(jump[:, :], pattern=[[0, E]], base=N, channel_multiplier=0,
                      allow_small_or_imprecise_dtypes=True).then_inc(pool_setup, 1)
            pool.wait_ge(pool_setup, 4)
            pool.affine_select(out=ident[:, :], in_=ident[:, :], compare_op=ALU.not_equal, fill=1.0, base=0,
                               pattern=[[-1, P]], channel_multiplier=1).then_inc(pool_setup, 1)

            def gather(r, k):
                if not isinstance(k, int) or k > 0:
                    pool.wait_ge(xT_filled, (k - 1) * LANES + r + 1)
                pool.wait_ge(idx_in[r], 16 * (k + 1))
                pool.sem_inc(passed, 1)
                pool.indirect_dma_start(out=xg[r][:, :], out_offset=None, in_=xn_rows[:, :],
                                        in_offset=bass.IndirectOffsetOnAxis(ap=idx[r][:, 0:1], axis=0)).then_inc(x_in[r], 16)

            for r in range(LANES):
                gather(r, 0)
            with pool.Fori(1, NT // LANES) as k:
                for r in range(LANES):
                    gather(r, k)

        def over_tiles(eng, step):
            for j in range(LANES):
                step(j, j, [j >= s for s in range(4)])
            with eng.Fori(1, NT // LANES) as k:
                for r in range(LANES):
                    step(k * LANES + r, r, [True] * 4)
            for j in range(NT, NT + 3):
                step(j, j % LANES, [j - s < NT for s in range(4)])

        @block.scalar
        def _(act):
            def step(j, r, on):
                if on[0]:
                    act.wait_ge(xT_filled, j + 1)
                    if not isinstance(j, int) or j >= 2:
                        act.wait_ge(gu_filled, j - 1)
                    act.activation(xT[r % 2][:, :, :].rearrange("p k t -> p (k t)"), psX[r % 2][:, 0:C],
                                   ACT.Copy).then_inc(xT_drained, 1)
                if on[1]:
                    q = (r - 1) % 2
                    act.wait_ge(gu_filled, j)
                    if not isinstance(j, int) or j >= 3:
                        act.wait_ge(h_ready, j - 2)
                    act.activation(sg[q][:, :], psGU[q][:, 0:I], ACT.Silu).then_inc(silu_ready, 1)
                if on[3]:
                    q = (r - 3) % 2
                    act.wait_ge(y_filled, j - 2)
                    lane = (r - 3) % LANES
                    if not isinstance(j, int) or j - 3 >= LANES:
                        act.wait_ge(y_saved[lane], rounds(j, r) * 16)
                    act.activation(yo[lane][:, :], psY[q][:, 0:C], ACT.Copy).then_inc(y_drained, 1)

            def rounds(j, r):
                if isinstance(j, int):
                    return (j - 3) // LANES
                return round_of[0] if r >= 3 else round_of[0] - 1

            round_of = [None]
            for j in range(LANES):
                step(j, j, [j >= s for s in range(4)])
            for r in range(LANES):
                step(LANES + r, r, [True] * 4)
            with act.Fori(2, NT // LANES) as k:
                round_of[0] = k
                for r in range(LANES):
                    step(k * LANES + r, r, [True] * 4)
            for j in range(NT, NT + 3):
                step(j, j % LANES, [j - s < NT for s in range(4)])

        @block.vector
        def _(dve):
            n = [0]

            def link(ins):
                n[0] += 1
                ins.then_inc(table_step, 1)
                dve.wait_ge(table_step, n[0])

            dve.wait_ge(pool_setup, 4)
            counts, starts = keep["counts"][:, :], keep["starts"][:, :]
            link(dve.tensor_copy(num[:, :], num_i[:, :]))
            link(dve.tensor_tensor(tiles[:, :], counts, starts, ALU.subtract))
            link(dve.tensor_scalar(tiles[:, :], tiles[:, :], float(P - 1), None, ALU.add))
            link(dve.tensor_copy(tiles_i[:, :], tiles[:, :]))
            link(dve.tensor_scalar(tiles_i[:, :], tiles_i[:, :], 7, None, ALU.logical_shift_right))
            link(dve.tensor_copy(tiles[:, :], tiles_i[:, :]))
            link(dve.tensor_copy(ends[0][:, :], tiles[:, :]))
            src = 0
            for d in (1, 2, 4, 8):
                link(dve.tensor_copy(ends[1 - src][:, 0:d], ends[src][:, 0:d]))
                link(dve.tensor_tensor(ends[1 - src][:, d:E], ends[src][:, d:E], ends[src][:, 0:E - d], ALU.add))
                src = 1 - src
            link(dve.scalar_tensor_tensor(out=jump[:, :], in0=tiles[:, :], scalar=-float(P), in1=jump[:, :],
                                          op0=ALU.mult, op1=ALU.add))
            bc = [1, NT, ER]
            link(dve.tensor_tensor(ge[:, :, :], num[:, :].unsqueeze(2).to_broadcast(bc),
                                   ends[src][0:1, 0:ER].unsqueeze(1).to_broadcast(bc), ALU.is_ge))
            link(dve.tensor_tensor(jumps[:, :, :], ge[:, :, :], jump[0:1, 0:ER].unsqueeze(1).to_broadcast(bc), ALU.mult))
            link(dve.tensor_reduce(expert[:, :], ge[:, :, :], axis=AX, op=ALU.add))
            link(dve.tensor_reduce(offset[:, :], jumps[:, :, :], axis=AX, op=ALU.add))
            link(dve.scalar_tensor_tensor(out=offset[:, :], in0=num[:, :], scalar=float(P), in1=offset[:, :],
                                          op0=ALU.mult, op1=ALU.add))
            link(dve.tensor_scalar(offset[:, :], offset[:, :], float(ER * N), None, ALU.min))
            link(dve.tensor_scalar(expert[:, :], expert[:, :], float(ER - 1), None, ALU.min))
            dve.tensor_copy(rows_i[:, :], offset[:, :]).then_inc(rows_ready, 1)
            link(dve.tensor_scalar(table[:, 1:NT + 1, 0], expert[:, :], float(ALLW), None, ALU.mult))
            dve.tensor_scalar(table[:, 3:NT + 3, 1], expert[:, :], float(ALLW), None, ALU.mult).then_inc(table_ready, 1)
            bc = [P, ROWS, ER]
            link(dve.tensor_tensor(past[:, :, :], row.unsqueeze(2).to_broadcast(bc),
                                   starts[:, 1:E].unsqueeze(1).to_broadcast(bc), ALU.is_ge))
            link(dve.tensor_tensor(past[:, :, :], past[:, :, :], jump[:, 0:ER].unsqueeze(1).to_broadcast(bc), ALU.mult))
            link(dve.tensor_reduce(back[:, :], past[:, :, :], axis=AX, op=ALU.add))
            link(dve.tensor_scalar(spare_row[:, :], ends[src][:, ER - 1:ER], float(P), None, ALU.mult))
            link(dve.tensor_tensor(back[:, :], row, back[:, :], ALU.subtract))
            link(dve.tensor_scalar(row, back[:, :], spare_row[:, 0:1], None, ALU.min))

            def step(j, r, on):
                if on[1]:
                    q = (r - 1) % 2
                    dve.wait_ge(silu_ready, j)
                    if not isinstance(j, int) or j >= 3:
                        dve.wait_ge(hT_filled, j - 2)
                    dve.tensor_tensor(hh[q][:, :], sg[q][:, :], psGU[q][:, I:2 * I], ALU.mult).then_inc(h_ready, 1)
                if on[2]:
                    q = (r - 2) % 2
                    dve.wait_ge(hT_filled, j - 1)
                    if not isinstance(j, int) or j >= 4:
                        dve.wait_ge(y_filled, j - 3)
                    dve.tensor_copy(hT[q][:, :], psH[q][:, 0:P]).then_inc(hT_drained, 1)

            over_tiles(dve, step)

        @block.tensor
        def _(pe):
            pe.wait_ge(weights_in, 16 * 5)
            pe.wait_ge(pool_setup, 5)
            pe.wait_ge(table_ready, 1)
            flat = weights[:, :, :].rearrange("p e w -> p (e w)")

            def lookup(j, column):
                return pe.value_load(table[0:1, bass.ds(j, 1), column], min_val=0, max_val=(ER - 1) * ALLW)

            at = [None] * LANES

            def step(j, r, on):
                if r == 0:
                    at[0] = lookup(j, 0)
                if on[0]:
                    if not isinstance(j, int) or j >= 2:
                        pe.wait_ge(xT_drained, j - 1)
                    k = j if isinstance(j, int) else None
                    pe.wait_ge(x_in[r], 16 * (j // LANES + 1) if k is not None else 16 * (round_of[0] + 1))
                    for c in range(KC):
                        last = pe.transpose(psX[r % 2][:, c * P:(c + 1) * P], xg[r][:, c * P:(c + 1) * P], ident[:, :])
                    last.then_inc(xT_filled, 1)
                if on[1]:
                    q = (r - 1) % 2
                    pe.wait_ge(xT_drained, j)
                    if not isinstance(j, int) or j >= 3:
                        pe.wait_ge(h_ready, j - 2)
                    for c in range(KC):
                        last = pe.matmul(psGU[q][:, 0:2 * I], xT[q][:, c, :], flat[:, bass.ds(at[r] + c * 2 * I, 2 * I)],
                                         start=(c == 0), stop=(c == KC - 1))
                    last.then_inc(gu_filled, 1)
                if on[3]:
                    down_at = at[r - 2] if r >= 2 else lookup(j, 1)
                if on[2]:
                    q = (r - 2) % 2
                    pe.wait_ge(h_ready, j - 1)
                    if not isinstance(j, int) or j >= 4:
                        pe.wait_ge(hT_drained, j - 3)
                    pe.transpose(psH[q][:, 0:P], hh[q][:, :], ident[:, :]).then_inc(hT_filled, 1)
                if on[3]:
                    q = (r - 3) % 2
                    pe.wait_ge(hT_drained, j - 2)
                    if not isinstance(j, int) or j >= 5:
                        pe.wait_ge(y_drained, j - 4)
                    pe.matmul(psY[q][:, 0:C], hT[q][:, :], flat[:, bass.ds(down_at + KC * 2 * I, C)], start=True,
                              stop=True).then_inc(y_filled, 1)
                if r < LANES - 1:
                    at[r + 1] = lookup(j + 1, 0)

            round_of = [None]
            for j in range(LANES):
                step(j, j, [j >= s for s in range(4)])
            for r in range(LANES):
                step(LANES + r, r, [True] * 4)
            with pe.Fori(2, NT // LANES) as k:
                round_of[0] = k
                for r in range(LANES):
                    step(k * LANES + r, r, [True] * 4)
            for j in range(NT, NT + 3):
                step(j, j % LANES, [j - s < NT for s in range(4)])


def combine_phase(nc, x1s, g_ffn, W, sc, keep, out):
    B, T, C = out.shape
    QT, KC = T // P, C // P
    I = W["shared_up_w"].shape[1]
    TAPS = W["conv_w"].shape[2]
    PAD = TAPS - 1
    xn_rows, results = sc["xn_rows"], sc["results"]
    with ExitStack() as st:
        def sb(name, shape, dt=F32):
            return st.enter_context(nc.sbuf_tensor(name, shape, dt))

        def ps(name):
            return st.enter_context(nc.psum_tensor(name, [P, 512], F32))

        def sem(name):
            return st.enter_context(nc.semaphore(name))

        passed = sem("passed_combine")
        psT = [ps(f"d_psT{k}") for k in range(KC)]
        psG, psU = ps("psG"), ps("psU")
        psD = [ps(f"psD{i}") for i in range(2)]
        at = [sb(f"at{i}", [P, QT, C]) for i in range(2)]
        xn = [sb(f"d_xn{i}", [P, QT, C]) for i in range(2)]
        xT = sb("d_xT", [P, KC, PAD + T])
        th, h = sb("th", [P, T]), sb("hsh", [P, T])
        conv_raw = sb("conv_raw", [P, C, TAPS])
        conv = sb("conv", [P, KC, TAPS, I])
        up = sb("shared_up", [P, KC, I])
        down = sb("shared_down", [P, C])
        gate = sb("d_gate", [P, 1])
        ident = sb("d_ident", [P, P])
        got = [sb(f"got{i}", [P, 2, QT, C]) for i in range(2)]
        rows = [sb(f"rows{i}", [P, 2 * QT], U32) for i in range(2)]
        w = [sb(f"wt{i}", [P, 3, QT]) for i in range(2)]

        loaded, pool_setup, vec_setup = sem("d_loaded"), sem("d_pool_setup"), sem("d_vec_setup")
        pe_setup, gate_ready = sem("d_pe_setup"), sem("d_gate_ready")
        x1_in = [sem(f"d_x1_in{i}") for i in range(2)]
        xn_in = [sem(f"d_xn_in{i}") for i in range(2)]
        xT_filled, xT_drained = sem("d_xT_filled"), sem("d_xT_drained")
        gu_filled, tanh_ready, silu_ready, h_ready = sem("d_gu"), sem("tanh_ready"), sem("silu_gate"), sem("d_h_ready")
        down_filled, term_added, done = sem("down_filled"), sem("term_added"), sem("d_done")
        rows_ready = sem("d_rows_ready")
        got_in = [sem(f"got_in{i}") for i in range(2)]
        saved = [sem(f"d_saved{i}") for i in range(2)]
        NL = 4
        block = st.enter_context(nc.Block())

        def over_batches(eng, body):
            body("pro", 0, 0)
            body("first", 0, 0)
            with eng.Fori(0, (B - 2) // 2) as i:
                body("mid", 2 * i + 1, 1)
                body("mid", 2 * i + 2, 0)
            body("last", B - 1, 1)

        def flags(kind):
            return kind != "pro", kind != "last"

        def after(kind, b):
            return 0 if kind == "pro" else b + 1

        def loads(b, par):
            return 8 * (b - par) + 16

        @block.sync
        def _(sp):
            def load_xn(b, par):
                sp.dma_start(xn[par][:, :, :], xn_rows.rearrange("(b t p) c -> b p t c", p=P, t=QT)[b]).then_inc(xn_in[par], 16)

            def load_x1(b, par):
                sp.dma_start(at[par][:, :, :], x1s[b].rearrange("(t p) c -> p t c", p=P)).then_inc(x1_in[par], 16)

            def body(b, par, two_ahead):
                if two_ahead:
                    sp.wait_ge(xT_filled, 2 * b + 2)
                    sp.wait_ge(term_added, 3 * b + 1)
                    load_xn(b + 2, par)
                sp.wait_ge(done, 2 * b + 2)
                sp.dma_start(out[b].rearrange("(t p) c -> p t c", p=P), at[par][:, :, :]).then_inc(saved[par], 16)
                if two_ahead:
                    sp.wait_ge(saved[par], loads(b, par))
                    load_x1(b + 2, par)

            sp.dma_start(conv_raw[:, :, :], W["conv_w"]).then_inc(loaded, 16)
            load_xn(0, 0)
            load_x1(0, 0)
            sp.dma_start(up[:, :, :], W["shared_up_w"].rearrange("(k p) i -> p k i", p=P)).then_inc(loaded, 16)
            sp.dma_start(down[:, :], W["shared_down_w"]).then_inc(loaded, 16)
            sp.dma_start(gate[:, :], g_ffn.partition_broadcast(P)).then_inc(loaded, 16)
            load_xn(1, 1)
            load_x1(1, 1)
            with sp.Fori(0, B // 2 - 1) as i:
                body(2 * i, 0, True)
                body(2 * i + 1, 1, True)
            for i in range(2):
                body(B - 2 + i, i, False)
            for i in range(2):
                sp.wait_ge(saved[i], 16 * B // 2)

        @block.gpsimd
        def _(pool):
            pool.memset(ident[:, :], 0.0).then_inc(pool_setup, 1)
            pool.memset(xT[:, :, 0:PAD], 0.0).then_inc(pool_setup, 1)
            pool.wait_ge(pool_setup, 2)
            pool.affine_select(out=ident[:, :], in_=ident[:, :], compare_op=ALU.not_equal, fill=1.0, base=0,
                               pattern=[[-1, P]], channel_multiplier=1).then_inc(pool_setup, 1)
            with pool.Fori(0, B // 2) as k:
                for i in range(2):
                    pool.wait_ge(rows_ready, 2 * k + i + 1)
                    pool.sem_inc(passed, 1)
                    for m in range(2):
                        for t in range(QT):
                            c = m * QT + t
                            pool.indirect_dma_start(
                                out=got[i][:, m, t, :], out_offset=None, in_=results[:, :],
                                in_offset=bass.IndirectOffsetOnAxis(ap=rows[i][:, c:c + 1], axis=0)).then_inc(got_in[i], 16)

        @block.scalar
        def _(act):
            act.wait_ge(loaded, 16 * NL)
            act.activation(gate[:, :], gate[:, :], ACT.Tanh).then_inc(gate_ready, 1)

            def body(kind, b, par):
                cur, nxt = flags(kind)
                n = after(kind, b)
                if cur:
                    act.wait_ge(gu_filled, b + 1)
                    if kind != "first":
                        act.wait_ge(h_ready, b)
                    act.activation(th[:, :], psG[:, :], ACT.Tanh, scale=0.5).then_inc(tanh_ready, 1)
                if nxt:
                    for k in range(KC):
                        act.wait_ge(xT_filled, 2 * n + k + 1)
                        act.activation(xT[:, k, PAD:], psT[k][:, :], ACT.Copy).then_inc(xT_drained, 1)

            over_batches(act, body)

        @block.vector
        def _(dve):
            dve.wait_ge(gate_ready, 1)
            dve.tensor_scalar(down[:, :], down[:, :], gate[:, 0:1], 0.5, ALU.mult, ALU.mult).then_inc(vec_setup, 1)
            dve.wait_ge(pe_setup, 1)
            for k in range(KC):
                dve.tensor_copy(conv[:, k, :, :].rearrange("p a i -> p (a i)"), psT[k][:, 0:TAPS * I]).then_inc(vec_setup, 1)

            def rows_of(b, i):
                dve.tensor_copy(w[i][:, 0, :], keep["identity"][:, bass.ds(b * QT, QT)])
                dve.tensor_copy(w[i][:, 1:3, :], keep["weight"][:, bass.ds(b * QT, QT), :].rearrange("p t k -> p k t"))
                dve.tensor_copy(rows[i][:, :].rearrange("p (m t) -> p m t", m=2),
                                keep["row"][:, bass.ds(b * 2, 2), :]).then_inc(rows_ready, 1)

            def term(i, m, src):
                for t in range(QT):
                    last = dve.scalar_tensor_tensor(out=at[i][:, t, :], in0=src[:, t, :], scalar=w[i][:, m, t:t + 1],
                                                    in1=at[i][:, t, :], op0=ALU.mult, op1=ALU.add)
                last.then_inc(term_added, 1)

            def body(b, par, two_ahead):
                dve.wait_ge(rows_ready, b + 1)
                dve.wait_ge(x1_in[par], loads(b, par))
                dve.wait_ge(xn_in[par], loads(b, par))
                term(par, 0, xn[par])
                dve.wait_ge(tanh_ready, b + 1)
                dve.scalar_tensor_tensor(out=h[:, :], in0=th[:, :], scalar=1.0, in1=psG[:, :],
                                         op0=ALU.add, op1=ALU.mult).then_inc(silu_ready, 1)
                dve.wait_ge(silu_ready, b + 1)
                dve.tensor_tensor(h[:, :], h[:, :], psU[:, :], ALU.mult).then_inc(h_ready, 1)
                dve.wait_ge(got_in[par], 2 * QT * loads(b, par))
                for m in range(2):
                    dve.wait_ge(term_added, 3 * b + m + 1)
                    term(par, m + 1, got[par][:, m, :, :])
                dve.wait_ge(term_added, 3 * b + 3)
                if two_ahead:
                    rows_of(b + 2, par)
                for i in range(2):
                    dve.wait_ge(down_filled, 2 * b + i + 1)
                    d = at[par][:, 2 * i:2 * i + 2, :].rearrange("p t c -> p (t c)")
                    dve.tensor_tensor(d, psD[i][:, :], d, ALU.add).then_inc(done, 1)

            for i in range(2):
                rows_of(i, i)
            with dve.Fori(0, B // 2 - 1) as k:
                for i in range(2):
                    body(2 * k + i, i, True)
            for i in range(2):
                body(B - 2 + i, i, False)

        @block.tensor
        def _(pe):
            pe.wait_ge(loaded, 16 * NL)
            pe.wait_ge(pool_setup, 3)
            for k in range(KC):
                for a in range(TAPS):
                    last = pe.transpose(psT[k][:, a * I:(a + 1) * I], conv_raw[:, k * P:(k + 1) * P, a], ident[:, :])
            last.then_inc(pe_setup, 1)
            pe.wait_ge(vec_setup, 1 + KC)

            def body(kind, b, par):
                cur, nxt = flags(kind)
                n = after(kind, b)
                if cur:
                    pe.wait_ge(xT_drained, 2 * n)
                    if kind != "first":
                        pe.wait_ge(h_ready, b)
                    for a in range(TAPS):
                        for k in range(KC):
                            pe.matmul(psG[:, :], conv[:, k, a, :], xT[:, k, a:a + T], start=(a == 0 and k == 0),
                                      stop=(a == TAPS - 1 and k == KC - 1))
                    for k in range(KC):
                        last = pe.matmul(psU[:, :], up[:, k, :], xT[:, k, PAD:], start=(k == 0), stop=(k == KC - 1))
                    last.then_inc(gu_filled, 1)
                if nxt:
                    q = 1 - par if cur else 0
                    pe.wait_ge(xn_in[q], loads(n, q))
                    for k in range(KC):
                        for t in range(QT):
                            last = pe.transpose(psT[k][:, t * P:(t + 1) * P], xn[q][:, t, k * P:(k + 1) * P], ident[:, :])
                        last.then_inc(xT_filled, 1)
                if cur:
                    pe.wait_ge(h_ready, b + 1)
                    if kind != "first":
                        pe.wait_ge(done, 2 * b)
                    for i in range(2):
                        for t in range(2):
                            last = pe.matmul(psD[i][:, t * C:(t + 1) * C], h[:, (2 * i + t) * P:(2 * i + t + 1) * P],
                                             down[:, :], start=True, stop=True)
                        last.then_inc(down_filled, 1)

            over_batches(pe, body)


def flamingo_gated_block(nc, x, ctx_512, g_xattn, g_ffn, Wk, bk, Wq, bq, Wv, bv, Wck, bck, Wcq, bcq, Wcv, bcv, Wp, bp,
                         router_w, router_bias, expert_gate_w, expert_up_w, expert_down_w, conv_w, shared_up_w,
                         shared_down_w, out):
    B, T, C = x.shape
    N, QT, E = B * T, T // P, router_w.shape[1]
    attention = dict(Wk=Wk, bk=bk, Wq=Wq, bq=bq, Wv=Wv, bv=bv, Wck=Wck, bck=bck, Wcq=Wcq, bcq=bcq, Wcv=Wcv, bcv=bcv,
                     Wp=Wp, bp=bp)
    ffn = dict(router_w=router_w, router_bias=router_bias, expert_gate_w=expert_gate_w, expert_up_w=expert_up_w,
               expert_down_w=expert_down_w, conv_w=conv_w, shared_up_w=shared_up_w, shared_down_w=shared_down_w)

    def dram(name, shape, dt=F32):
        return nc.dram_tensor(name, shape, dt, kind="Internal").ap()

    x1 = dram("x1", (B, T, C))
    scratch = dict(
        xn_rows=dram("xn_rows", (N, C)),
        lists=dram("lists", (E * N + 2 * QT * P, 1), I32),
        results=dram("results", (expert_tiles(N, E - 1) * P, C)))

    with ExitStack() as st:
        keep = dict(weight=st.enter_context(nc.sbuf_tensor("keep_weight", [P, B * QT, 2], F32)),
                    identity=st.enter_context(nc.sbuf_tensor("keep_identity", [P, B * QT], F32)),
                    row=st.enter_context(nc.sbuf_tensor("keep_row", [P, B * 2, QT], F32)),
                    counts=st.enter_context(nc.sbuf_tensor("keep_counts", [P, E], F32)),
                    starts=st.enter_context(nc.sbuf_tensor("keep_starts", [P, E], F32)))
        attention_phase(nc, x, ctx_512, g_xattn, attention, x1, g_ffn, router_w, router_bias, scratch["xn_rows"],
                        scratch["lists"], keep)
        expert_phase(nc, ffn, scratch, keep, N)
        combine_phase(nc, x1, g_ffn, ffn, scratch, keep, out)


_INS = ['x', 'ctx_512', 'g_xattn', 'g_ffn', 'L0_xattn_Wk', 'L0_xattn_bk', 'L0_xattn_Wq', 'L0_xattn_bq', 'L0_xattn_Wv',
        'L0_xattn_bv', 'L0_xattn_Wck', 'L0_xattn_bck', 'L0_xattn_Wcq', 'L0_xattn_bcq', 'L0_xattn_Wcv', 'L0_xattn_bcv',
        'L0_xattn_Wp', 'L0_xattn_bp', 'L0_ffn_router_w', 'L0_ffn_router_bias', 'L0_ffn_expert_gate_w',
        'L0_ffn_expert_up_w', 'L0_ffn_expert_down_w', 'L0_ffn_conv_w', 'L0_ffn_shared_up_w', 'L0_ffn_shared_down_w']
_OUTS = [((16, 512, 256), 'float32')]


def kernel(**inputs):
    import numpy as _np
    import concourse.bacc as _bacc
    from concourse import mybir as _mybir
    from concourse.bass_utils import run_bass_kernel_spmd as _run

    nc = _bacc.Bacc("TRN2", target_bir_lowering=False, num_devices=1)
    arrays, args = {}, []
    for name in _INS:
        a = _np.ascontiguousarray(inputs[name])
        arrays[f"in_{name}_dram"] = a
        args.append(nc.dram_tensor(f"in_{name}_dram", a.shape, _mybir.dt.from_np(a.dtype), kind="ExternalInput").ap())
    for i, (shape, dtype) in enumerate(_OUTS):
        dt = _mybir.dt.from_np(_np.dtype(dtype))
        args.append(nc.dram_tensor(f"out_{i}_dram", shape, dt, kind="ExternalOutput").ap())
    flamingo_gated_block(nc, *args)
    r = _run(nc, [arrays], core_ids=[0])
    return r.results[0]["out_0_dram"]
```
